# Optimizing a Trainium2 kernel written in Bass

```python
import numpy as np
import jax
import jax.numpy as jnp

def _softmax(x, axis=-1):
    return jax.nn.softmax(x, axis=axis)

def _gelu(x):
    return jax.nn.gelu(x, approximate=True)

def _silu(x):
    return jax.nn.silu(x)

def _sigmoid(x):
    return jax.nn.sigmoid(x)

def _layernorm(x, axis=-1, eps=1e-05):
    m = jnp.mean(x, axis=axis, keepdims=True)
    v = jnp.var(x, axis=axis, keepdims=True)
    return (x - m) / jnp.sqrt(v + eps)

def _scatter_add(tgt, idx, src, axis=0):
    return tgt.at[idx].add(src)

def _segment_sum(src, seg, n):
    return jax.ops.segment_sum(src, seg, n)
kernel_name = 'mk_gnn_resnorm_d4_gnn_r8_efe94e'

def setup_inputs(seed: int=0):
    np.random.seed(seed)
    _w = jnp.asarray

    def _rec_inputs():
        import jax
        import jax.numpy as jnp
        _gk = jax.random.key(seed)
        x = -0.0003713 + 1 * jax.random.normal(jax.random.fold_in(_gk, 1), (6250, 128), jnp.float32)
        src = jax.random.randint(jax.random.fold_in(_gk, 2), (200000,), 0, 6250, jnp.int32)
        dst = jnp.minimum((6250 * jax.random.uniform(jax.random.fold_in(_gk, 3), (200000,)) ** 2.0).astype(jnp.int32), 49999)
        _o = jnp.argsort(dst, stable=True)
        src = src[_o]
        dst = dst[_o]
        edge_attr_3 = 0.00011001 + 1.00018 * jax.random.normal(jax.random.fold_in(_gk, 11), (200000, 3), jnp.float32)
        edge_weight = jax.random.uniform(jax.random.fold_in(_gk, 13), (200000,), jnp.float32, 0.0, 0.999999)
        return (x, src, dst, edge_attr_3, edge_weight)
    x, src, dst, edge_attr_3, edge_weight = _rec_inputs()

    def _L0_gnn_setup():
        import jax, jax.numpy as jnp
        import numpy as np
        N_NODES = 12500
        N_CLIQUES = 6250
        N_EDGES = 200000
        D_IN = 128
        D_OUT = 128
        key = jax.random.key(seed)
        k1, k2, k3, k4, k5, k6 = jax.random.split(key, 6)
        x = jax.random.normal(k1, (N_NODES, D_IN), dtype=jnp.float32)
        x_clique = jax.random.normal(k2, (N_CLIQUES, D_IN), dtype=jnp.float32)
        node_idx = jax.random.randint(k3, (N_EDGES,), 0, N_NODES, dtype=jnp.int64)
        clique_idx = jax.random.randint(k4, (N_EDGES,), 0, N_CLIQUES, dtype=jnp.int64)
        node2clique_index = jnp.stack([node_idx, clique_idx], axis=0)
        W = jax.random.normal(k5, (D_OUT, D_IN), dtype=jnp.float32) * (1.0 / np.sqrt(D_IN))
        b = jax.random.normal(k6, (D_OUT,), dtype=jnp.float32) * 0.01
        return {'x': x, 'x_clique': x_clique, 'node2clique_index': node2clique_index, 'W': W, 'b': b}
    _L0_gnn_all = _L0_gnn_setup()
    _L0_gnn_in = {k: v for k, v in _L0_gnn_all.items() if k in ('x_clique', 'W', 'b')}
    del _L0_gnn_all

    def _L1_gnn_setup():
        import jax, jax.numpy as jnp
        import numpy as np
        N = 12500
        E = 400000
        F_IN = 128
        F_OUT = 128
        key = jax.random.key(seed)
        k1, k2, k3, k4 = jax.random.split(key, 4)
        x = jax.random.normal(k1, (N, F_IN), dtype=jnp.float32)
        edge_index = jax.random.randint(k2, (2, E), 0, N, dtype=jnp.int64)
        W = jax.random.normal(k3, (F_IN, F_OUT), dtype=jnp.float32) * 0.05
        b = jax.random.normal(k4, (F_OUT,), dtype=jnp.float32) * 0.05
        return {'x': x, 'edge_index': edge_index, 'W': W, 'b': b}
    _L1_gnn_all = _L1_gnn_setup()
    _L1_gnn_in = {k: v for k, v in _L1_gnn_all.items() if k in ('W', 'b')}
    del _L1_gnn_all

    def _L2_gnn_setup():
        import jax, jax.numpy as jnp
        import numpy as np
        N, E0, F_IN, HEADS, C = (6250, 100000, 128, 4, 32)
        HC = HEADS * C
        NEG_SLOPE = 0.2

        def gatv2_block(x, edge_index, lin_l_w, lin_l_b, lin_r_w, lin_r_b, att, conv_bias, lin_w, lin_b, bn_gamma, bn_beta):
            n = x.shape[0]
            xl = (x @ lin_l_w.T + lin_l_b).reshape(n, HEADS, C)
            xr = (x @ lin_r_w.T + lin_r_b).reshape(n, HEADS, C)
            ar = jnp.arange(n, dtype=edge_index.dtype)
            src = jnp.concatenate([edge_index[0], ar])
            dst = jnp.concatenate([edge_index[1], ar])
            m = jax.nn.leaky_relu(xl[src] + xr[dst], NEG_SLOPE)
            alpha = jnp.sum(m * att, axis=-1)
            amax = jax.ops.segment_max(alpha, dst, num_segments=n)
            ealpha = jnp.exp(alpha - amax[dst])
            denom = jax.ops.segment_sum(ealpha, dst, num_segments=n)
            w = ealpha / (denom[dst] + 1e-16)
            out = jax.ops.segment_sum(xl[src] * w[:, :, None], dst, num_segments=n)
            h = out.reshape(n, HC) + conv_bias
            h = jax.nn.relu(h)
            mu = jnp.mean(h, axis=0)
            var = jnp.mean(jnp.square(h - mu), axis=0)
            h = (h - mu) * jax.lax.rsqrt(var + 1e-05) * bn_gamma + bn_beta
            return h @ lin_w.T + lin_b
        key = jax.random.key(seed)
        ks = jax.random.split(key, 12)
        x = jax.random.normal(ks[0], (N, F_IN), dtype=jnp.float32)
        src = jax.random.randint(ks[1], (E0,), 0, N)
        off = jax.random.randint(ks[2], (E0,), 1, N)
        dst = (src + off) % N
        edge_index = jnp.stack([src, dst]).astype(jnp.int64)
        edge_attr = jax.random.uniform(ks[3], (E0,), dtype=jnp.float32)
        s = 1.0 / np.sqrt(F_IN)
        lin_l_w = jax.random.uniform(ks[4], (HC, F_IN), minval=-s, maxval=s)
        lin_l_b = jnp.zeros((HC,), jnp.float32)
        lin_r_w = jax.random.uniform(ks[5], (HC, F_IN), minval=-s, maxval=s)
        lin_r_b = jnp.zeros((HC,), jnp.float32)
        att = jax.random.normal(ks[6], (1, HEADS, C)) * 0.1
        conv_bias = jnp.zeros((HC,), jnp.float32)
        s2 = 1.0 / np.sqrt(HC)
        lin_w = jax.random.uniform(ks[7], (HC, HC), minval=-s2, maxval=s2)
        lin_b = jax.random.uniform(ks[8], (HC,), minval=-s2, maxval=s2)
        bn_gamma = jnp.ones((HC,), jnp.float32)
        bn_beta = jnp.zeros((HC,), jnp.float32)
        return dict(x=x, edge_index=edge_index, edge_attr=edge_attr, lin_l_w=lin_l_w, lin_l_b=lin_l_b, lin_r_w=lin_r_w, lin_r_b=lin_r_b, att=att, conv_bias=conv_bias, lin_w=lin_w, lin_b=lin_b, bn_gamma=bn_gamma, bn_beta=bn_beta)
    _L2_gnn_all = _L2_gnn_setup()
    _L2_gnn_in = {k: v for k, v in _L2_gnn_all.items() if k in ('lin_l_w', 'lin_l_b', 'lin_r_w', 'lin_r_b', 'att', 'conv_bias', 'lin_w', 'lin_b', 'bn_gamma', 'bn_beta')}
    del _L2_gnn_all

    def _L3_gnn_setup():
        import jax, jax.numpy as jnp
        import numpy as np
        T, D, E, DE = (6250, 128, 200000, 3)
        EPS = 1e-05
        key = jax.random.key(seed)
        ks = jax.random.split(key, 8)
        H = jax.random.normal(ks[0], (T, D), dtype=jnp.float32)
        edge_index = jax.random.randint(ks[1], (2, E), 0, T, dtype=jnp.int64)
        edge_attr = jax.random.normal(ks[2], (E, DE), dtype=jnp.float32)
        s1 = 1.0 / np.sqrt(D + DE)
        s2 = 1.0 / np.sqrt(D)
        W1 = jax.random.uniform(ks[3], (D + DE, D), minval=-s1, maxval=s1, dtype=jnp.float32)
        b1 = jax.random.uniform(ks[4], (D,), minval=-s1, maxval=s1, dtype=jnp.float32)
        W2 = jax.random.uniform(ks[5], (D, D), minval=-s2, maxval=s2, dtype=jnp.float32)
        b2 = jax.random.uniform(ks[6], (D,), minval=-s2, maxval=s2, dtype=jnp.float32)
        gamma = jnp.ones((D,), dtype=jnp.float32)
        beta = jnp.zeros((D,), dtype=jnp.float32)
        return {'H': H, 'edge_index': edge_index, 'edge_attr': edge_attr, 'W1': W1, 'b1': b1, 'W2': W2, 'b2': b2, 'gamma': gamma, 'beta': beta}
    _L3_gnn_all = _L3_gnn_setup()
    _L3_gnn_in = {k: v for k, v in _L3_gnn_all.items() if k in ('W1', 'b1', 'W2', 'b2', 'gamma', 'beta')}
    del _L3_gnn_all
    return {'x': x, 'src': src, 'dst': dst, 'edge_attr_3': edge_attr_3, 'edge_weight': edge_weight, 'L0_gnn_x_clique': _L0_gnn_in['x_clique'], 'L0_gnn_W': _L0_gnn_in['W'], 'L0_gnn_b': _L0_gnn_in['b'], 'L1_gnn_W': _L1_gnn_in['W'], 'L1_gnn_b': _L1_gnn_in['b'], 'L2_gnn_lin_l_w': _L2_gnn_in['lin_l_w'], 'L2_gnn_lin_l_b': _L2_gnn_in['lin_l_b'], 'L2_gnn_lin_r_w': _L2_gnn_in['lin_r_w'], 'L2_gnn_lin_r_b': _L2_gnn_in['lin_r_b'], 'L2_gnn_att': _L2_gnn_in['att'], 'L2_gnn_conv_bias': _L2_gnn_in['conv_bias'], 'L2_gnn_lin_w': _L2_gnn_in['lin_w'], 'L2_gnn_lin_b': _L2_gnn_in['lin_b'], 'L2_gnn_bn_gamma': _L2_gnn_in['bn_gamma'], 'L2_gnn_bn_beta': _L2_gnn_in['bn_beta'], 'L3_gnn_W1': _L3_gnn_in['W1'], 'L3_gnn_b1': _L3_gnn_in['b1'], 'L3_gnn_W2': _L3_gnn_in['W2'], 'L3_gnn_b2': _L3_gnn_in['b2'], 'L3_gnn_gamma': _L3_gnn_in['gamma'], 'L3_gnn_beta': _L3_gnn_in['beta']}

def reference(x, src, dst, edge_attr_3, edge_weight, L0_gnn_x_clique, L0_gnn_W, L0_gnn_b, L1_gnn_W, L1_gnn_b, L2_gnn_lin_l_w, L2_gnn_lin_l_b, L2_gnn_lin_r_w, L2_gnn_lin_r_b, L2_gnn_att, L2_gnn_conv_bias, L2_gnn_lin_w, L2_gnn_lin_b, L2_gnn_bn_gamma, L2_gnn_bn_beta, L3_gnn_W1, L3_gnn_b1, L3_gnn_W2, L3_gnn_b2, L3_gnn_gamma, L3_gnn_beta):
    import jax
    import jax.numpy as jnp

    def _L0_gnn_ref(x, x_clique, node2clique_index, W, b):
        import jax, jax.numpy as jnp
        import numpy as np
        N_NODES = 12500
        N_CLIQUES = 6250
        N_EDGES = 200000
        D_IN = 128
        D_OUT = 128
        node_idx = node2clique_index[0]
        clique_idx = node2clique_index[1]
        n_nodes = x.shape[0]
        gathered = x_clique[clique_idx]
        summed = jax.ops.segment_sum(gathered, node_idx, num_segments=n_nodes)
        count = jax.ops.segment_sum(jnp.ones((gathered.shape[0],), dtype=x_clique.dtype), node_idx, num_segments=n_nodes)
        mean = summed / jnp.maximum(count, 1.0)[:, None]
        out = mean @ W.T + b
        return out

    def _L1_gnn_ref(x, edge_index, W, b):
        import jax, jax.numpy as jnp
        import numpy as np
        N = 12500
        E = 400000
        F_IN = 128
        F_OUT = 128
        num_nodes = x.shape[0]
        loop = jnp.arange(num_nodes, dtype=edge_index.dtype)
        row = jnp.concatenate([edge_index[0], loop])
        col = jnp.concatenate([edge_index[1], loop])
        deg = jax.ops.segment_sum(jnp.ones_like(row, dtype=x.dtype), row, num_segments=num_nodes)
        deg_inv_sqrt = jnp.where(deg > 0, jax.lax.rsqrt(deg), 0.0)
        norm = deg_inv_sqrt[row] * deg_inv_sqrt[col]
        h = x @ W + b
        msgs = h[col] * norm[:, None]
        out = jax.ops.segment_sum(msgs, row, num_segments=num_nodes)
        return out

    def _L2_gnn_ref(x, edge_index, edge_attr, lin_l_w, lin_l_b, lin_r_w, lin_r_b, att, conv_bias, lin_w, lin_b, bn_gamma, bn_beta):
        import jax, jax.numpy as jnp
        import numpy as np
        N, E0, F_IN, HEADS, C = (6250, 100000, 128, 4, 32)
        HC = HEADS * C
        NEG_SLOPE = 0.2

        def gatv2_block(x, edge_index, lin_l_w, lin_l_b, lin_r_w, lin_r_b, att, conv_bias, lin_w, lin_b, bn_gamma, bn_beta):
            n = x.shape[0]
            xl = (x @ lin_l_w.T + lin_l_b).reshape(n, HEADS, C)
            xr = (x @ lin_r_w.T + lin_r_b).reshape(n, HEADS, C)
            ar = jnp.arange(n, dtype=edge_index.dtype)
            src = jnp.concatenate([edge_index[0], ar])
            dst = jnp.concatenate([edge_index[1], ar])
            m = jax.nn.leaky_relu(xl[src] + xr[dst], NEG_SLOPE)
            alpha = jnp.sum(m * att, axis=-1)
            amax = jax.ops.segment_max(alpha, dst, num_segments=n)
            ealpha = jnp.exp(alpha - amax[dst])
            denom = jax.ops.segment_sum(ealpha, dst, num_segments=n)
            w = ealpha / (denom[dst] + 1e-16)
            out = jax.ops.segment_sum(xl[src] * w[:, :, None], dst, num_segments=n)
            h = out.reshape(n, HC) + conv_bias
            h = jax.nn.relu(h)
            mu = jnp.mean(h, axis=0)
            var = jnp.mean(jnp.square(h - mu), axis=0)
            h = (h - mu) * jax.lax.rsqrt(var + 1e-05) * bn_gamma + bn_beta
            return h @ lin_w.T + lin_b
        return gatv2_block(x, edge_index, lin_l_w, lin_l_b, lin_r_w, lin_r_b, att, conv_bias, lin_w, lin_b, bn_gamma, bn_beta)

    def _L3_gnn_ref(H, edge_index, edge_attr, W1, b1, W2, b2, gamma, beta):
        import jax, jax.numpy as jnp
        import numpy as np
        T, D, E, DE = (6250, 128, 200000, 3)
        EPS = 1e-05
        src, dst = (edge_index[0], edge_index[1])
        Hj = H[src]
        feat = jnp.concatenate([Hj, edge_attr], axis=-1)
        h = jax.nn.gelu(feat @ W1 + b1, approximate=False)
        m = h @ W2 + b2
        agg = jax.ops.segment_sum(m, dst, num_segments=H.shape[0])
        x = H + agg
        mu = jnp.mean(x, axis=-1, keepdims=True)
        var = jnp.mean((x - mu) ** 2, axis=-1, keepdims=True)
        return (x - mu) * jax.lax.rsqrt(var + EPS) * gamma + beta
    edge_index = jnp.stack([src, dst])
    x = _layernorm(x + _L0_gnn_ref(x, L0_gnn_x_clique, edge_index, L0_gnn_W, L0_gnn_b), axis=-1)
    x = _layernorm(x + _L1_gnn_ref(x, edge_index, L1_gnn_W, L1_gnn_b), axis=-1)
    x = _layernorm(x + _L2_gnn_ref(x, edge_index, edge_weight, L2_gnn_lin_l_w, L2_gnn_lin_l_b, L2_gnn_lin_r_w, L2_gnn_lin_r_b, L2_gnn_att, L2_gnn_conv_bias, L2_gnn_lin_w, L2_gnn_lin_b, L2_gnn_bn_gamma, L2_gnn_bn_beta), axis=-1)
    x = _layernorm(x + _L3_gnn_ref(x, edge_index, edge_attr_3, L3_gnn_W1, L3_gnn_b1, L3_gnn_W2, L3_gnn_b2, L3_gnn_gamma, L3_gnn_beta), axis=-1)
    return x

_drawn_inputs = setup_inputs


def setup_inputs(seed=0):
    import zlib

    import numpy as np

    out = dict(_drawn_inputs(seed))
    spreads = {'L2_gnn_lin_l_b': (0.0, 0.1),
     'L2_gnn_lin_r_b': (0.0, 0.8),
     'L2_gnn_conv_bias': (0.0, 0.1),
     'L2_gnn_bn_gamma': (1.0, 0.2),
     'L2_gnn_bn_beta': (0.0, 0.1),
     'L3_gnn_gamma': (1.0, 0.2),
     'L3_gnn_beta': (0.0, 0.1)}
    factors = {}
    for name, (base, spread) in spreads.items():
        noise = np.random.default_rng([zlib.crc32(name.encode()), seed]).standard_normal(out[name].shape)
        drawn = base * np.exp(spread * noise) if base else spread * noise
        out[name] = jnp.asarray(drawn.astype(out[name].dtype))
    for name, factor in factors.items():
        out[name] = (out[name] * factor).astype(out[name].dtype)
    return out
```

```python
from contextlib import ExitStack

import concourse.bass as bass
from concourse import mybir

F32 = mybir.dt.float32
I32 = mybir.dt.int32
BF16 = mybir.dt.bfloat16
ALU = mybir.AluOpType
ACT = mybir.ActivationFunctionType
AX = mybir.AxisListType
ET = mybir.EngineType

P = 128
D = 128
N = 6250
E = 200000
H, C = 4, 32
FULL = N // P
REST = N - FULL * P
NB = 49
NW = NB + 1
NC = 1568
LASTC = E - (P - 1) * NC
PADNODE = NB * P - 1
PAIR = 2 * P
BODY = 8
NP = -(-((P * NC + NB * (PAIR - 1)) // PAIR + 1) // BODY) * BODY
T = 2 * NP
WS, WD = 4, 8
AW = D + H
ONE = D
EPS = 1e-5
LOW = -1e30
RING = 4
CONSTS = 9
FILLS = 6
BIG = max(NB * H * P, NW * AW + NC * (WS + WD))


def gnn_kernel(nc, a, out):
    with ExitStack() as ctx:
        def sb(name, shape, dt=F32):
            return ctx.enter_context(nc.sbuf_tensor(name, shape, dt))

        def sem(name):
            return ctx.enter_context(nc.semaphore(name))

        recs_dram = nc.dram_tensor("recs_dram", [P, T, WS], F32).ap()
        recd_dram = nc.dram_tensor("recd_dram", [P, T, WD], F32).ap()
        tab1 = nc.dram_tensor("tab1", [NW * P, D], F32).ap()
        tab2 = nc.dram_tensor("tab2", [NW * P, D], F32).ap()
        tab3 = nc.dram_tensor("tab3", [NW * P, D], F32).ap()
        rows2 = nc.dram_tensor("rows2", [P, NP, 2 * D], F32).ap()

        x = sb("x", [P, NW, D])
        xr = sb("xr", [P, NW, D])
        big = sb("big", [P, BIG])
        alp = sb("alp", [P, T * H])
        acc = big[:, 0:NW * AW].rearrange("p (w f) -> p w f", w=NW)
        zself = big[:, 0:NW * D].rearrange("p (w f) -> p w f", w=NW)
        rmax = big[:, 0:NB * H * P].rearrange("p (w f) -> p w f", w=NB)
        tmp = alp[:, 0:NW * D].rearrange("p (w f) -> p w f", w=NW)
        alpha = alp[:].rearrange("p (j c) -> p j c", j=NP)
        eself = big[:, NW * AW:NW * AW + NW * H]
        o = NW * AW
        recd = big[:, o:o + NC * WD].rearrange("p (c w) -> p c w", w=WD)
        recs = big[:, o + NC * WD:o + NC * (WD + WS)].rearrange("p (c w) -> p c w", w=WS)
        srci = alp[:, 0:NC].bitcast(I32)
        dsti = alp[:, NC:2 * NC].bitcast(I32)
        mask = alp[:, 2 * NC:3 * NC]
        scan = alp[:, 3 * NC:4 * NC]
        xflat = x[:].rearrange("p w f -> p (w f)")
        xrflat = xr[:].rearrange("p w f -> p (w f)")
        FT = T // 10
        filld = xflat[:, 0:FT * WD].rearrange("p (t w) -> p t w", w=WD)
        fills = xflat[:, FT * WD:FT * (WD + WS)].rearrange("p (t w) -> p t w", w=WS)
        o = FT * (WD + WS)
        key = xflat[:, o:o + NC]
        pos = xflat[:, o + NC:o + 2 * NC]
        ea = xrflat[:, 0:3 * NC]
        wraw = xrflat[:, 3 * NC:3 * NC + 4 * D].rearrange("p (k f) -> p k f", k=4)
        iotap = xrflat[:, 3 * NC + 4 * D:3 * NC + 4 * D + NP]
        ltri = xrflat[:, 3 * NC + 4 * D + NP:3 * NC + 4 * D + NP + P]

        ident = sb("ident", [P, P])
        ones = sb("ones", [P, P])
        iota = sb("iota", [P, P])
        iotab = sb("iotab", [P, P], BF16)
        identb = sb("identb", [P, P], BF16)
        bids = sb("bids", [65, NP], I32)
        rows = bids[64:65, 0:6 * D].bitcast(F32)
        rec = sb("rec", [P, 4, 4, WD])
        recs4 = rec[:].rearrange("p k t (a w) -> p (k t a) w", a=2)
        g = sb("g", [P, RING, 2, AW])
        oh = sb("oh", [P, RING, 2, P])
        pen = oh[:].rearrange("p a u d -> p (a u d)").bitcast(BF16).rearrange("p (a u d) -> p a u d", a=BODY, u=2)
        oht = sb("oht", [P, 2, PAIR])
        zt = sb("zt", [P, 2, PAIR])
        msg = sb("msg", [P, 2, 2, AW])
        xb = sb("xb", [P, 2, D])
        w01 = sb("w01", [P, 2 * D])
        w0t, w1 = w01[:, 0:D], w01[:, D:2 * D]
        ohb = w01[:].bitcast(BF16).rearrange("p (a u d) -> p a u d", a=2, u=2)
        wlrt = sb("wlrt", [P, 2 * D])
        lint = sb("lint", [P, D])
        w31 = sb("w31", [P, D])
        w32 = sb("w32", [P, D])
        w31b = sb("w31b", [2 * WD, 2, D])
        attm = sb("attm", [P, H])
        bc = sb("bc", [P, 2, D])
        cnt = sb("cnt", [P, NW])
        dinv = sb("dinv", [P, NW])
        st = sb("st", [P, 4, NW])
        aself = sb("aself", [P, NW * H])
        amax = sb("amax", [P, NW * H])
        ea8 = sb("ea8", [P, 2, 2 * H])
        lt = msg[:].rearrange("p a u f -> p (a u f)")[:, 0:2 * PAIR].rearrange("p (a e) -> p a e", a=2)
        rfix = g[:].rearrange("p a u f -> p (a u f)")[:, 0:2 * H * P].rearrange("p (a f) -> p a f", a=2)

        ps = ctx.enter_context(nc.psum_tensor("ps", [P, 8, 512], F32))

        ntab = lambda t: t.rearrange("(w p) f -> p w f", p=P)

        s_const = sem("const_made")
        s_load = sem("weights_in")
        s_edges = sem("edges_in")
        s_fill = sem("fill_made")
        s_filled = sem("records_filled")
        s_pad = sem("pad_made")
        s_ea = sem("attributes_in")
        s_eac = sem("attributes_placed")
        s_wt = sem("weight_transposed")
        s_wtc = sem("weight_copied")
        s_v = sem("vector_chain")
        s_cnt = sem("window_counts")
        s_pre = sem("window_prefixes")
        s_cum = sem("window_starts")
        s_cmp = sem("pair_windows_compared")
        s_cmpd = sem("pair_windows_summed")
        s_rank = sem("rows_ranked")
        s_stage = [sem(f"staged{h}") for h in range(2)]
        s_scat = [sem(f"scattered{h}") for h in range(2)]
        s_x = sem("x_in")
        s_pc, s_pt, s_pa, s_pm, s_pe = (sem(f"project_{n}") for n in ("copied", "turned", "turned_copied", "product", "out"))
        ready = {n: sem(f"ready_{n}") for n in (
            "x_zero", "l0_mean", "l1_in", "l1_rows", "l2_in", "l2_left", "l2_go", "l2_sums", "l2_sums_done",
            "l2_conv_bias_used", "l2_norm", "l3_in", "l3_rows", "l3_sums", "l3_b2_used", "out")}
        s_sq = sem("squares_ready")
        s_sd = sem("roots_ready")
        s_tab = sem("table_stored")
        s_vec = sem("vectors_in")
        s_bn = sem("batch_sums")
        s_done = sem("out_stored")
        s_cmpr = sem("pair_windows_kept")
        b_dif = sem("l2b_difference_made")
        s_clear = sem("pool_cleared")
        s_exs = sem("self_weights_made")
        s_rc, s_rt, s_rr = sem("max_copied"), sem("max_turned"), sem("max_reduced")
        s_bng = sem("batch_operand_ready")

        class Pass:
            def __init__(self, name):
                self.rec = [sem(f"{name}_records_in{k}") for k in range(4)]
                self.got = [sem(f"{name}_rows_in{k}") for k in range(RING)]
                self.oh = sem(f"{name}_onehot_made")
                self.used = sem(f"{name}_rows_used")
                self.acc = sem(f"{name}_sums_added")

        pa0, pa1, pa2, pb2, pa3 = (Pass(n) for n in ("l0", "l1", "l2a", "l2b", "l3"))
        s_kept = [sem(f"l2a_rows_kept{k}") for k in range(RING)]
        s_tr = sem("l2a_onehot_turned")
        s_trc = sem("l2a_onehot_turned_copied")
        s_zc = sem("l2a_sum_copied")
        s_lr = sem("l2a_leaky_made")
        s_al = sem("l2a_logits_made")
        s_alc = sem("l2a_logits_kept")
        s_rm = sem("l2a_max_updated")
        b_tr = sem("l2b_onehot_turned")
        b_trc = sem("l2b_onehot_turned_copied")
        b_sh = sem("l2b_shift_made")
        b_sub = sem("l2b_logits_shifted")
        b_exp = sem("l2b_weights_made")
        b_msg = sem("l2b_messages_made")
        c_tr = sem("l3_records_turned")
        c_trc = sem("l3_records_turned_copied")
        c_z = sem("l3_hidden_made")
        c_msg = sem("l3_gelu_made")

        def steps(eng, n, unroll, stages, regs=None):
            def load(first, count, lag_reg=None):
                e, bid_row = regs[0], regs[1]
                return nc.values_load_multi_w_load_instructions(
                    bid_row[:, first] if isinstance(first, slice) else bid_row[:, bass.ds(first, count)],
                    engines=[e], min_val=0, max_val=NB - 1,
                    skip_runtime_bounds_check_because="a pair's window is clamped to the last one")[1]
            most = max(lag for lag, _ in stages)
            rlag = regs[2] if regs else 0

            def call(f, i, q, w):
                f(i, q) if w is None else f(i, q, w)

            w = load(0, unroll - rlag) if regs else None
            for q in range(unroll):
                for lag, f in stages:
                    if q >= lag:
                        call(f, 0, q - lag, w[q - lag] if regs and lag == rlag and f.__name__.endswith("_w") else None)
            with eng.Fori(1, n // unroll) as i:
                w = load(i * unroll - rlag, unroll) if regs else None
                for q in range(unroll):
                    for lag, f in stages:
                        call(f, i if q >= lag else i - 1, (q - lag) % unroll,
                             w[q] if regs and f.__name__.endswith("_w") else None)
            if most:
                w = load(n - rlag, rlag) if regs and rlag else None
                for q in range(most):
                    for lag, f in stages:
                        if lag > q:
                            call(f, n // unroll - 1, unroll + q - lag, w[q] if regs and f.__name__.endswith("_w") else None)

        def later(i, q, unroll, r):
            return not isinstance(i, int) or i * unroll + q >= r

        def row(t, w):
            return t[:, bass.ds(w, 1), :].rearrange("p a f -> p (a f)")

        block = ctx.enter_context(nc.Block())


        def project_act(k, src, act):
            base = NW * k

            def fix(i, q):
                w = i * 2 + q
                if k or later(i, q, 2, 2):
                    act.wait_ge(s_pt, base + w - 1)
                nc.scalar.activation(xb[:, q, :], row(src, w), ACT.Copy).then_inc(s_pc, 1)

            def turned(i, q):
                w = i * 2 + q
                act.wait_ge(s_pt, base + w + 1)
                if k or later(i, q, 2, 2):
                    act.wait_ge(s_pm, base + w - 1)
                nc.scalar.activation(zt[:, q, 0:P], ps[:, q, 0:P], ACT.Copy).then_inc(s_pa, 1)
            steps(act, NW, 2, [(0, fix), (1, turned)])

        def project_pe(k, wt, m, b, pe):
            base = NW * k

            def turn(i, q):
                w = i * 2 + q
                pe.wait_ge(s_pc, base + w + 1)
                if k or later(i, q, 2, 2):
                    pe.wait_ge(s_pa, base + w - 1)
                nc.tensor.transpose(ps[:, q, 0:P], xb[:, q, :], ident[:]).then_inc(s_pt, 1)

            def product(i, q):
                w = i * 2 + q
                pe.wait_ge(s_pa, base + w + 1)
                if k or later(i, q, 2, 2):
                    pe.wait_ge(s_pe, base + w - 1)
                last = nc.tensor.matmul(ps[:, 2 + q, 0:m], zt[:, q, 0:P], wt[:, 0:m], start=True, stop=b is None)
                if b is not None:
                    last = nc.tensor.matmul(ps[:, 2 + q, 0:m], ones[64:65, :], rows[:, b * D:b * D + m], start=False, stop=True)
                last.then_inc(s_pm, 1)
            steps(pe, NW, 2, [(0, turn), (1, product)])

        def project_dve(k, dsts, dve):
            base = NW * k

            def leave(i, q):
                w = i * 2 + q
                dve.wait_ge(s_pm, base + w + 1)
                for n, dst in enumerate(dsts):
                    last = nc.vector.tensor_copy(row(dst, w), ps[:, 2 + q, n * D:n * D + D])
                last.then_inc(s_pe, 1)
            steps(dve, NW, 2, [(0, leave)])

        def record(k, t, words):
            return rec[:, k, t, :] if words == WD else rec[:, k, t // 2, WS * (t % 2):WS * (t % 2) + WS]

        def records(k, words):
            return rec[:, k, :, :] if words == WD else rec[:, k, 0:2, :].rearrange("p t (a w) -> p (t a) w", a=2)

        @block.sync
        def _(sp):
            sp.wait_ge(s_pad, 2)
            for t, name in ((srci, "src"), (dsti, "dst")):
                v = a[name][0:(P - 1) * NC].rearrange("(p c) -> p c", c=NC)
                sp.dma_start(t[0:112, :], v[0:112, :]).then_inc(s_edges, 16)
                sp.dma_start(t[112:P - 1, :], v[112:P - 1, :]).then_inc(s_edges, 16)
                sp.dma_start(t[P - 1:P, 0:LASTC],
                             a[name][(P - 1) * NC:E].rearrange("(p c) -> p c", p=1)).then_inc(s_edges, 16)
            v = a["edge_attr_3"][0:(P - 1) * NC, :].rearrange("(p c) k -> p (c k)", c=NC)
            sp.dma_start(ea[0:112, :], v[0:112, :]).then_inc(s_ea, 16)
            sp.dma_start(ea[112:P - 1, :], v[112:P - 1, :]).then_inc(s_ea, 16)
            sp.dma_start(ea[P - 1:P, 0:3 * LASTC],
                         a["edge_attr_3"][(P - 1) * NC:E, :].rearrange("(p c) k -> p (c k)", p=1)).then_inc(s_ea, 16)
            for dst, src in ((wraw[:, 0, :], a["L0_gnn_W"]), (wraw[:, 1, :], a["L2_gnn_lin_l_w"]),
                             (wraw[:, 2, :], a["L2_gnn_lin_r_w"]), (wraw[:, 3, :], a["L2_gnn_lin_w"]),
                             (w1, a["L1_gnn_W"]), (w31[:], a["L3_gnn_W1"][0:D, :]), (w32[:], a["L3_gnn_W2"])):
                sp.dma_start(dst, src).then_inc(s_load, 16)
            for n, name in enumerate(("L0_gnn_b", "L1_gnn_b", "L2_gnn_lin_l_b", "L2_gnn_lin_r_b", "L2_gnn_lin_b",
                                      "L3_gnn_b1")):
                sp.dma_start(rows[:, n * D:n * D + D], a[name].rearrange("(p f) -> p f", p=1)).then_inc(s_load, 16)
            sp.wait_ge(s_const, CONSTS)
            for u in range(2):
                sp.dma_start(w31b[u * WD + 2:u * WD + 5, u, :], a["L3_gnn_W1"][D:D + 3, :]).then_inc(s_load, 16)
            for h in range(H):
                sp.dma_start(attm[C * h:C * h + C, h:h + 1],
                             a["L2_gnn_att"][0, h, :].rearrange("(c b) -> c b", b=1)).then_inc(s_load, 16)
            sp.wait_ge(s_fill, FILLS)
            for k in range(10):
                sp.dma_start(recd_dram[:, k * FT:k * FT + FT, :], filld).then_inc(s_filled, 16)
                sp.dma_start(recs_dram[:, k * FT:k * FT + FT, :], fills).then_inc(s_filled, 16)

            def stage(order, src, words):
                sp.wait_ge(s_rank, order + 1)

                def move(i, h):
                    if order or later(i, h, 2, 2):
                        sp.wait_ge(s_scat[h], 64 * (order * NC // 8 + i))
                    sp.dma_start(records(h, words), src[:, bass.ds(i * 8 + 4 * h, 4), :]).then_inc(s_stage[h], 16)
                steps(sp, NC // 4, 2, [(0, move)])
            stage(0, recs, WS)
            sp.wait_ge(s_eac, 3)
            stage(1, recd, WD)
            sp.wait_ge(ready["x_zero"], 1)
            sp.dma_start(x[:, 0:FULL, :], a["x"][0:FULL * P, :].rearrange("(w p) f -> p w f", p=P)).then_inc(s_x, 16)
            sp.dma_start(x[0:REST, FULL, :], a["x"][FULL * P:N, :]).then_inc(s_x, 16)
            for h in range(2):
                sp.wait_ge(s_scat[h], 64 * 2 * NC // 8)

            def stream(pas, dram, words):
                def load(i, k):
                    sp.dma_start(records(k, words), dram[:, bass.ds((i * BODY + 2 * k) * 2, 4), :]).then_inc(pas.rec[k], 16)
                for k in range(4):
                    load(0, k)
                with sp.Fori(1, NP // BODY) as i:
                    for k in range(4):
                        sp.wait_ge(pas.used, i * BODY + 2 * k + 2 - BODY)
                        load(i, k)
            stream(pa0, recs_dram, WS)
            sp.wait_ge(ready["l1_rows"], 1)
            sp.dma_start(ntab(tab1), xr[:]).then_inc(s_tab, 16)
            stream(pa1, recs_dram, WS)
            sp.dma_start(bc[:, 0, :], a["L2_gnn_att"].rearrange("a h c -> (a h c)").partition_broadcast(P)).then_inc(s_vec, 16)
            sp.wait_ge(ready["l2_left"], 1)
            sp.dma_start(ntab(tab2), tmp).then_inc(s_tab, 16)

            def load2(pas, i, k):
                sp.dma_start(records(k, WD), recd_dram[:, bass.ds((i * BODY + 2 * k) * 2, 4), :]).then_inc(pas.rec[k], 16)

            def keep(i, q):
                s = q % RING
                sp.wait_ge(pa2.got[s], 32 * (i * 2 + q // RING + 1))
                sp.dma_start(rows2[:, bass.ds(i * BODY + q, 1), :].rearrange("p a (t f) -> p (a t) f", t=2),
                             g[:, s, :, 0:D]).then_inc(s_kept[s], 16)

            def reload(i, q):
                sp.wait_ge(pa2.oh, i * BODY + q + 1)
                load2(pa2, i + 1, q // 2)
            for k in range(4):
                load2(pa2, 0, k)
            last = NP // BODY - 1
            for q in range(BODY):
                keep(0, q)
                if q in (3, 5, 7):
                    reload(0, q - 2)
            with sp.Fori(1, last) as i:
                for q in range(BODY):
                    keep(i, q)
                    if q == 1:
                        reload(i - 1, BODY - 1)
                    elif q % 2 == 1:
                        reload(i, q - 2)
            for q in range(BODY):
                keep(last, q)
                if q == 1:
                    reload(last - 1, BODY - 1)
            for s in range(RING):
                sp.wait_ge(s_kept[s], 16 * NP // RING)

            sp.wait_ge(ready["l2_sums"], 1)

            def again(i, q):
                s = q % RING
                if q % 2 == 0:
                    if later(i, q, BODY, BODY):
                        sp.wait_ge(pb2.oh, i * BODY + q + 2 - BODY)
                    load2(pb2, i, q // 2)
                if later(i, q, BODY, RING):
                    sp.wait_ge(b_msg, i * BODY + q - RING + 1)
                sp.dma_start(g[:, s, :, 0:D], rows2[:, bass.ds(i * BODY + q, 1), :].rearrange("p a (t f) -> p (a t) f", t=2))\
                    .then_inc(pb2.got[s], 16)
            steps(sp, NP, BODY, [(0, again)])
            sp.wait_ge(ready["l2_sums_done"], 1)
            sp.dma_start(tmp, ntab(tab2)).then_inc(s_tab, 16)
            for n, name in enumerate(("L2_gnn_conv_bias", "L2_gnn_bn_gamma")):
                sp.dma_start(bc[:, n, :], a[name].partition_broadcast(P)).then_inc(s_vec, 16)
            sp.wait_ge(ready["l2_conv_bias_used"], 1)
            sp.dma_start(bc[:, 0, :], a["L2_gnn_bn_beta"].partition_broadcast(P)).then_inc(s_vec, 16)
            sp.wait_ge(ready["l3_rows"], 1)
            sp.dma_start(ntab(tab3), xr[:]).then_inc(s_tab, 16)
            sp.dma_start(bc[:, 0, :], a["L3_gnn_b2"].partition_broadcast(P)).then_inc(s_vec, 16)
            sp.dma_start(bc[:, 1, :], a["L3_gnn_gamma"].partition_broadcast(P)).then_inc(s_vec, 16)
            stream(pa3, recd_dram, WD)
            sp.wait_ge(ready["l3_b2_used"], 1)
            sp.dma_start(bc[:, 0, :], a["L3_gnn_beta"].partition_broadcast(P)).then_inc(s_vec, 16)
            sp.wait_ge(ready["out"], 1)
            sp.dma_start(out[0:FULL * P, :].rearrange("(w p) f -> p w f", p=P), x[:, 0:FULL, :]).then_inc(s_done, 16)
            sp.dma_start(out[FULL * P:N, :], x[0:REST, FULL, :]).then_inc(s_done, 16)
            sp.wait_ge(s_done, 32)

        @block.gpsimd
        def _(pool):
            gp = nc.gpsimd
            gp.memset(srci, PADNODE).then_inc(s_pad, 1)
            gp.memset(dsti, PADNODE).then_inc(s_pad, 1)
            gp.memset(recs, 0.0).then_inc(s_fill, 1)
            gp.memset(recd, 0.0).then_inc(s_fill, 1)
            gp.memset(filld, 0.0).then_inc(s_fill, 1)
            gp.memset(fills, 0.0).then_inc(s_fill, 1)
            pool.wait_ge(s_fill, 4)
            gp.memset(filld[:, :, 1:2], -1.0).then_inc(s_fill, 1)
            gp.memset(fills[:, :, 1:2], -1.0).then_inc(s_fill, 1)
            gp.memset(ident[:], 0.0).then_inc(s_const, 1)
            gp.memset(ones[:], 1.0).then_inc(s_const, 1)
            gp.iota(iota[:], [[1, P]], base=0, channel_multiplier=0, allow_small_or_imprecise_dtypes=True).then_inc(s_const, 1)
            gp.memset(w31b[:], 0.0).then_inc(s_const, 1)
            gp.memset(attm[:], 0.0).then_inc(s_const, 1)
            gp.memset(g[:, :, :, ONE:ONE + 1], 1.0).then_inc(s_const, 1)
            gp.iota(iotap, [[1, NP]], base=0, channel_multiplier=0, allow_small_or_imprecise_dtypes=True).then_inc(s_const, 1)
            pool.wait_ge(s_const, CONSTS - 2)
            gp.affine_select(out=ident[:], in_=ident[:], compare_op=ALU.not_equal, fill=1.0, base=0,
                             pattern=[[-1, P]], channel_multiplier=1).then_inc(s_const, 1)
            gp.affine_select(out=ltri, in_=ones[:], compare_op=ALU.is_gt, fill=0.0, base=0,
                             pattern=[[1, P]], channel_multiplier=-1).then_inc(s_const, 1)

            def scatter(order, words, dram):
                table = dram.rearrange("p t w -> (p t) w")

                def tiles(i, h):
                    pool.wait_ge(s_stage[h], 16 * (order * NC // 8 + i + 1))
                    pool.sem_inc(s_clear, 1)
                    for t in range(4):
                        r = record(h, t, words)
                        gp.indirect_dma_start(
                            out=table, out_offset=bass.IndirectOffsetOnAxis(ap=r[:, words - 1:words].bitcast(I32), axis=0),
                            in_=r, in_offset=None).then_inc(s_scat[h], 16)
                steps(pool, NC // 4, 2, [(0, tiles)])

            def gathers(pas, words, table, kept=None):
                def pair(i, q):
                    s, k = q % RING, q // 2
                    if q % 2 == 0:
                        pool.wait_ge(pas.rec[k], 16 * (i + 1))
                    if later(i, q, BODY, RING):
                        pool.wait_ge(pas.used, i * BODY + q - RING + 1)
                        if kept is not None:
                            pool.wait_ge(kept[s], 16 * (i * 2 + q // RING))
                    pool.sem_inc(s_clear, 1)
                    for u in range(2):
                        gp.indirect_dma_start(
                            out=g[:, s, u, 0:D], out_offset=None, in_=table,
                            in_offset=bass.IndirectOffsetOnAxis(
                                ap=record(k, 2 * (q % 2) + u, words)[:, 0:1].bitcast(I32), axis=0)).then_inc(pas.got[s], 16)
                steps(pool, NP, BODY, [(0, pair)])

            pool.wait_ge(s_filled, 320)
            scatter(0, WS, recs_dram)
            scatter(1, WD, recd_dram)
            gathers(pa0, WS, a["L0_gnn_x_clique"])
            pool.wait_ge(s_tab, 16)
            gathers(pa1, WS, tab1)
            pool.wait_ge(s_tab, 32)
            gathers(pa2, WD, tab2, s_kept)
            pool.wait_ge(s_tab, 64)
            gathers(pa3, WD, tab3)

        @block.scalar
        def _(act):
            sc = nc.scalar
            act.wait_ge(s_ea, 48)
            act.wait_ge(s_fill, 4)
            ea3 = ea.rearrange("p (c k) -> p c k", k=3)
            sc.activation(recd[0:96, :, 2:5], ea3[0:96], ACT.Copy).then_inc(s_eac, 1)
            sc.activation(recd[96:P, 0:LASTC, 2:5], ea3[96:P, 0:LASTC], ACT.Copy).then_inc(s_eac, 1)
            sc.activation(recd[96:P - 1, LASTC:NC, 2:5], ea3[96:P - 1, LASTC:NC], ACT.Copy).then_inc(s_eac, 1)
            for k, dst in enumerate((w0t, wlrt[:, 0:D], wlrt[:, D:2 * D], lint[:])):
                act.wait_ge(s_wt, k + 1)
                sc.activation(dst, ps[:, k, 0:P], ACT.Copy).then_inc(s_wtc, 1)

            def roots(n):
                act.wait_ge(s_sq, n + 1)
                sc.activation(st[:, 3, :], st[:, 2, :], ACT.Sqrt).then_inc(s_sd, 1)

            roots(0)
            act.wait_ge(ready["l0_mean"], 1)
            project_act(0, acc[:, :, 0:D], act)
            roots(1)
            act.wait_ge(ready["l1_in"], 1)
            project_act(1, x, act)
            roots(2)
            act.wait_ge(ready["l2_in"], 1)
            project_act(2, x, act)

            act.wait_ge(ready["l2_go"], 1)

            def window_w(i, q, w):
                j = i * BODY + q
                if later(i, q, BODY, 2):
                    act.wait_ge(pa2.used, j - 1)
                sc.activation(xb[:, q % 2, :], row(xr, w), ACT.Copy)
                act.wait_ge(s_tr, j + 1)
                sc.activation(oht[:, q % 2, :], ps[:, q % 2, 0:P].bitcast(BF16), ACT.Copy).then_inc(s_trc, 1)

            def summed(i, q):
                j = i * BODY + q
                act.wait_ge(pa2.used, j + 1)
                if later(i, q, BODY, 2):
                    act.wait_ge(s_lr, j - 1)
                sc.activation(zt[:, q % 2, :], ps[:, 2 + q % 2, 0:PAIR], ACT.Copy).then_inc(s_zc, 1)

            def logits(i, q):
                j = i * BODY + q
                act.wait_ge(s_al, j + 1)
                sc.activation(alpha[:, bass.ds(j, 1), :].rearrange("p a c -> p (a c)"),
                              ps[:, 4 + q % 2, 0:2 * H], ACT.Copy).then_inc(s_alc, 1)
            steps(act, NP, BODY, [(0, window_w), (1, summed), (3, logits)], (ET.Activation, bids[32:33, :], 0))

            act.wait_ge(s_rm, 2 * H * NP)
            for s in range(RING):
                act.wait_ge(s_kept[s], 16 * NP // RING)

            def fixmax(i, q):
                w = i * 2 + q
                if later(i, q, 2, 2):
                    act.wait_ge(s_rt, w - 1)
                sc.activation(rfix[:, q, :], row(rmax, w), ACT.Copy).then_inc(s_rc, 1)
            steps(act, NB - 1, 2, [(0, fixmax)])
            fixmax(NB // 2, 0)

            act.wait_ge(ready["l2_sums"], 1)

            def turned(i, q):
                j = i * BODY + q
                act.wait_ge(b_tr, j + 1)
                if later(i, q, BODY, 2):
                    act.wait_ge(b_sh, j - 1)
                sc.activation(oht[:, q % 2, :], ps[:, q % 2, 0:PAIR], ACT.Copy).then_inc(b_trc, 1)

            def weights(i, q):
                j = i * BODY + q
                act.wait_ge(b_sub, j + 1)
                if later(i, q, BODY, 2):
                    act.wait_ge(pb2.used, j - 1)
                sc.activation(msg[:, q % 2, :, D:AW], ea8[:, q % 2, :].rearrange("p (t h) -> p t h", t=2),
                              ACT.Exp).then_inc(b_exp, 1)
            steps(act, NP, BODY, [(0, turned), (2, weights)])
            act.wait_ge(ready["l2_sums_done"], 1)
            sc.activation(eself, eself, ACT.Exp).then_inc(s_exs, 1)
            act.wait_ge(s_sq, 4)
            sc.activation(msg[:, 0, 1, 0:D], msg[:, 0, 0, 0:D], ACT.Sqrt).then_inc(s_sd, 1)
            act.wait_ge(ready["l2_norm"], 1)
            project_act(3, tmp, act)
            roots(4)
            act.wait_ge(ready["l3_in"], 1)
            project_act(4, x, act)

            act.wait_ge(ready["l3_rows"], 1)

            def turned3(i, q):
                j = i * BODY + q
                act.wait_ge(c_tr, j + 1)
                if later(i, q, BODY, 2):
                    act.wait_ge(c_z, j - 1)
                sc.activation(zt[0:2 * WD, q % 2, 0:P], ps[0:2 * WD, q % 2, 0:P], ACT.Copy).then_inc(c_trc, 1)

            def gelu(i, q):
                j = i * BODY + q
                act.wait_ge(c_z, j + 1)
                if later(i, q, BODY, 2):
                    act.wait_ge(pa3.used, j - 1)
                sc.activation(msg[:, q % 2, :, 0:D], ps[:, 2 + q % 2, 0:PAIR].rearrange("p (t f) -> p t f", t=2),
                              ACT.Gelu).then_inc(c_msg, 1)
            steps(act, NP, BODY, [(0, turned3), (1, gelu)])
            act.wait_ge(ready["l3_sums"], 1)
            project_act(5, acc[:, :, 0:D], act)
            roots(5)
            roots(6)

        @block.tensor
        def _(pe):
            mm = nc.tensor.matmul
            pe.wait_ge(s_load, 19 * 16)
            pe.wait_ge(s_const, CONSTS)
            for k in range(4):
                nc.tensor.transpose(ps[:, k, 0:P], wraw[:, k, :], ident[:]).then_inc(s_wt, 1)
            for order in range(2):
                pe.wait_ge(s_cnt, order + 1)
                if order:
                    pe.wait_ge(s_cmpr, 1)
                mm(ps[:, 4, 0:NB], ltri, cnt[:, 0:NB], start=True, stop=True)
                mm(ps[:, 5, 0:NB], ones[:], cnt[:, 0:NB], start=True, stop=True).then_inc(s_pre, 1)
                pe.wait_ge(s_cum, order + 1)
                mm(ps[0:NB, 6, 0:1], st[0:1, 2, 0:NB], ones[0:1, 0:1], start=True, stop=True).then_inc(s_pre, 1)
                pe.wait_ge(s_cmp, order + 1)
                for n in range(2):
                    last = mm(ps[0:1, 4 + n, 0:NP // 2], ones[0:NB - 1, 0:1], mask[0:NB - 1, n * NP // 2:(n + 1) * NP // 2],
                              start=True, stop=True)
                last.then_inc(s_cmpd, 1)

            def plain_pass(pas):
                def sums(i, q):
                    j = i * BODY + q
                    pe.wait_ge(pas.oh, j + 1)
                    pe.wait_ge(pas.got[q % RING], 32 * (i * 2 + q // RING + 1))
                    if later(i, q, BODY, 2):
                        pe.wait_ge(pas.acc, j - 1)
                    for u in range(2):
                        last = mm(ps[:, 6 + q % 2, 0:D + 1], oh[:, q % RING, u, :], g[:, q % RING, u, 0:D + 1],
                                  start=(u == 0), stop=(u == 1))
                    last.then_inc(pas.used, 1)
                steps(pe, NP, BODY, [(0, sums)])

            plain_pass(pa0)
            pe.wait_ge(s_wtc, 4)
            project_pe(0, w0t, D, 0, pe)
            project_pe(1, w1, D, 1, pe)
            pe.wait_ge(ready["l1_rows"], 1)
            plain_pass(pa1)
            project_pe(2, wlrt, 2 * D, 2, pe)

            pe.wait_ge(ready["l2_go"], 1)

            def turn(i, q):
                j = i * BODY + q
                pe.wait_ge(pa2.oh, j + 1)
                if later(i, q, BODY, 2):
                    pe.wait_ge(s_trc, j - 1)
                for u in range(2):
                    last = nc.tensor.transpose(ps[:, q % 2, 0:P].bitcast(BF16)[:, u * P:u * P + P], ohb[:, q % 2, u, :], identb[:])
                last.then_inc(s_tr, 1)

            def add(i, q):
                j = i * BODY + q
                pe.wait_ge(s_trc, j + 1)
                pe.wait_ge(pa2.got[q % RING], 32 * (i * 2 + q // RING + 1))
                if later(i, q, BODY, 2):
                    pe.wait_ge(s_zc, j - 1)
                for u in range(2):
                    z = ps[:, 2 + q % 2, u * P:u * P + P]
                    mm(z, xb[:, q % 2, :], oht[:, q % 2, u * P:u * P + P], start=True, stop=False)
                    last = mm(z, g[:, q % RING, u, 0:D], ident[:], start=False, stop=True)
                last.then_inc(pa2.used, 1)

            def logit(i, q):
                j = i * BODY + q
                pe.wait_ge(s_lr, j + 1)
                if later(i, q, BODY, 2):
                    pe.wait_ge(s_alc, j - 1)
                    pe.wait_ge(s_rm, 2 * H * (j - 1))
                for u in range(2):
                    last = mm(ps[:, 4 + q % 2, u * H:u * H + H], lt[:, q % 2, u * P:u * P + P], attm[:],
                              start=True, stop=True)
                last.then_inc(s_al, 1)
            steps(pe, NP, BODY, [(0, turn), (1, add), (3, logit)])

            def turnmax(i, q):
                w = i * 2 + q
                pe.wait_ge(s_rc, w + 1)
                if later(i, q, 2, 2):
                    pe.wait_ge(s_rr, w - 1)
                for h in range(H):
                    last = nc.tensor.transpose(ps[:, q, h * P:h * P + P], rfix[:, q, h * P:h * P + P], ident[:])
                last.then_inc(s_rt, 1)
            steps(pe, NB - 1, 2, [(0, turnmax)])
            turnmax(NB // 2, 0)

            pe.wait_ge(ready["l2_sums"], 1)

            def turn_b(i, q):
                j = i * BODY + q
                pe.wait_ge(pb2.oh, j + 1)
                if later(i, q, BODY, 2):
                    pe.wait_ge(b_trc, j - 1)
                for u in range(2):
                    last = nc.tensor.transpose(ps[:, q % 2, u * P:u * P + P], oh[:, q % RING, u, :], ident[:])
                last.then_inc(b_tr, 1)

            def shift_w(i, q, w):
                j = i * BODY + q
                pe.wait_ge(b_trc, j + 1)
                if later(i, q, BODY, 2):
                    pe.wait_ge(b_sub, j - 1)
                for u in range(2):
                    last = mm(ps[:, 4 + q % 2, u * H:u * H + H], oht[:, q % 2, u * P:u * P + P],
                              amax[:, bass.ds(w * H, H)], start=True, stop=True)
                last.then_inc(b_sh, 1)

            def sums_b(i, q):
                j = i * BODY + q
                pe.wait_ge(b_msg, j + 1)
                if later(i, q, BODY, 2):
                    pe.wait_ge(pb2.acc, j - 1)
                for u in range(2):
                    last = mm(ps[:, 6 + q % 2, 0:AW], oh[:, q % RING, u, :], msg[:, q % 2, u, :], start=(u == 0), stop=(u == 1))
                last.then_inc(pb2.used, 1)
            steps(pe, NP, BODY, [(3, sums_b), (0, turn_b), (1, shift_w)], (ET.PE, bids[32:33, :], 1))

            for n, t in enumerate((tmp, xr)):
                pe.wait_ge(s_bng, n + 1)
                for w in range(FULL + 1):
                    k = P if w < FULL else REST
                    last = mm(ps[:, 4 + n, 0:D], ones[0:k, :], t[0:k, w, :], start=(w == 0), stop=(w == FULL))
                last.then_inc(s_bn, 1)
            project_pe(3, lint, D, 4, pe)
            project_pe(4, w31, D, 5, pe)

            pe.wait_ge(ready["l3_rows"], 1)

            def turn_c(i, q):
                j = i * BODY + q
                if q % 2 == 0:
                    pe.wait_ge(pa3.rec[q // 2], 16 * (i + 1))
                if later(i, q, BODY, 2):
                    pe.wait_ge(c_trc, j - 1)
                nc.tensor.transpose(ps[0:2 * WD, q % 2, 0:P],
                                    rec[:, q // 2, 2 * (q % 2):2 * (q % 2) + 2, :].rearrange("p t w -> p (t w)"),
                                    ident[:]).then_inc(c_tr, 1)

            def hidden(i, q):
                j = i * BODY + q
                pe.wait_ge(c_trc, j + 1)
                pe.wait_ge(pa3.got[q % RING], 32 * (i * 2 + q // RING + 1))
                if later(i, q, BODY, 2):
                    pe.wait_ge(c_msg, j - 1)
                mm(ps[:, 2 + q % 2, 0:PAIR], zt[0:2 * WD, q % 2, 0:P], w31b[:].rearrange("p u f -> p (u f)"),
                   start=True, stop=False)
                mm(ps[:, 2 + q % 2, 0:PAIR], ident[:], g[:, q % RING, :, 0:D], start=False, stop=True).then_inc(c_z, 1)

            def sums_c(i, q):
                j = i * BODY + q
                pe.wait_ge(c_msg, j + 1)
                pe.wait_ge(pa3.oh, j + 1)
                if later(i, q, BODY, 2):
                    pe.wait_ge(pa3.acc, j - 1)
                for u in range(2):
                    last = mm(ps[:, 6 + q % 2, 0:D + 1], oh[:, q % RING, u, :], msg[:, q % 2, u, 0:D + 1],
                              start=(u == 0), stop=(u == 1))
                last.then_inc(pa3.used, 1)
            steps(pe, NP, BODY, [(0, turn_c), (1, hidden), (2, sums_c)])
            project_pe(5, w32, D, None, pe)

        @block.vector
        def _(dve):
            v = nc.vector
            chained = [0]

            def link(ins):
                chained[0] += 1
                ins.then_inc(s_v, 1)
                dve.wait_ge(s_v, chained[0])

            def sort(order, by, other, recx, words):
                maski, scani, posi, keyi = (t.bitcast(I32) for t in (mask, scan, pos, key))
                v.tensor_scalar(maski, by, P - 1, None, ALU.bitwise_and)
                v.tensor_scalar(scani, by, 7, None, ALU.logical_shift_right)
                link(v.tensor_scalar(recx[:, :, 0:1].bitcast(I32).rearrange("p c w -> p (c w)"), other, N - 1, None, ALU.min))
                v.tensor_copy(recx[:, :, 1:2].rearrange("p c w -> p (c w)"), maski)
                link(v.tensor_copy(key, scani))
                for b in range(NB):
                    link(v.tensor_scalar(mask, key, float(b), 0.0, ALU.is_equal, ALU.add, accum_out=cnt[:, b:b + 1]))
                dve.sem_inc(s_cnt, 1)
                dve.wait_ge(s_pre, 2 * order + 1)
                sti = st[:, 0, 0:NB].bitcast(I32)
                link(v.tensor_scalar(sti, ps[:, 5, 0:NB], float(PAIR - 1), None, ALU.add))
                link(v.tensor_scalar(sti, sti, 8, None, ALU.logical_shift_right))
                link(v.tensor_copy(st[:, 1, 0:NB], sti))
                link(v.tensor_tensor_scan(st[:, 2, 0:NB], ones[:, 0:NB], st[:, 1, 0:NB], 0.0, ALU.mult, ALU.add))
                v.tensor_tensor(st[:, 1, 0:NB], st[:, 2, 0:NB], st[:, 1, 0:NB], ALU.subtract).then_inc(s_cum, 1)
                dve.wait_ge(s_cum, order + 1)
                link(v.scalar_tensor_tensor(st[:, 3, 0:NB], st[:, 1, 0:NB], float(PAIR), ps[:, 4, 0:NB], ALU.mult, ALU.add))
                dve.wait_ge(s_pre, 2 * order + 2)
                v.tensor_scalar(mask[0:NB - 1, 0:NP], iotap[0:NB - 1, :], ps[0:NB - 1, 6, 0:1], None, ALU.is_ge).then_inc(s_cmp, 1)
                dve.wait_ge(s_cmpd, order + 1)
                for n in range(2):
                    last = v.tensor_copy(bids[32 * order:32 * order + 1, n * NP // 2:(n + 1) * NP // 2], ps[0:1, 4 + n, 0:NP // 2])
                last.then_inc(s_cmpr, 1)
                link(v.memset(pos, 0.0))
                for b in range(NB):
                    link(v.tensor_scalar(mask, key, float(b), None, ALU.is_equal))
                    link(v.tensor_tensor_scan(scan, mask, mask, st[:, 3, b:b + 1], ALU.add, ALU.max))
                    link(v.copy_predicated(pos, maski, scan))
                link(v.tensor_scalar(scani, pos, -1.0, None, ALU.add))
                v.tensor_scalar(maski, scani, PAIR - 1, 1, ALU.bitwise_and, ALU.logical_shift_right)
                v.tensor_scalar(posi, scani, 8, 1, ALU.logical_shift_right, ALU.logical_shift_left)
                link(v.tensor_scalar(keyi, scani, 1, None, ALU.bitwise_and))
                link(v.tensor_tensor(posi, posi, keyi, ALU.bitwise_or))
                v.scalar_tensor_tensor(recx[:, :, words - 1:words].bitcast(I32).rearrange("p c w -> p (c w)"), maski, float(T),
                                       posi, ALU.mult, ALU.add).then_inc(s_rank, 1)
                dve.wait_ge(s_rank, order + 1)

            dve.wait_ge(s_edges, 96)
            dve.wait_ge(s_fill, FILLS)
            dve.wait_ge(s_const, CONSTS)
            dve.wait_ge(s_load, 19 * 16)
            v.tensor_copy(iotab[:], iota[:])
            v.tensor_copy(identb[:], ident[:])
            sort(0, srci, dsti, recs, WS)
            sort(1, dsti, srci, recd, WD)
            dve.wait_ge(s_eac, 3)
            dve.wait_ge(s_filled, 320)
            v.memset(x[:], 0.0).then_inc(ready["x_zero"], 1)
            v.memset(acc, 0.0)
            link(v.memset(st[:], 0.0))

            def onehots(pas, words, free):
                def onehot(i, q):
                    if q % 2 == 0:
                        dve.wait_ge(pas.rec[q // 2], 16 * (i + 1))
                    if later(i, q, BODY, RING):
                        free(i * BODY + q - RING + 1)
                    for u in range(2):
                        last = v.tensor_scalar(oh[:, q % RING, u, :], iota[:], record(q // 2, 2 * (q % 2) + u, words)[:, 1:2],
                                               None, ALU.is_equal)
                    last.then_inc(pas.oh, 1)
                return onehot

            def adds(pas, width):
                def add_w(i, q, w):
                    j = i * BODY + q
                    dve.wait_ge(pas.used, j + 1)
                    if later(i, q, BODY, 1):
                        dve.wait_ge(pas.acc, j)
                    v.tensor_tensor(row(acc, w)[:, 0:width], row(acc, w)[:, 0:width], ps[:, 6 + q % 2, 0:width],
                                    ALU.add).then_inc(pas.acc, 1)
                return add_w

            def plain_pass(pas, words, order, lag):
                free = lambda n: dve.wait_ge(pas.used, n)
                steps(dve, NP, BODY, [(0, onehots(pas, words, free)), (lag, adds(pas, D + 1))],
                      (ET.DVE, bids[32 * order:32 * order + 1, :], lag))
                dve.wait_ge(pas.acc, NP)

            wide = [P, NW, D]
            by_window = lambda t: t.unsqueeze(2).to_broadcast(wide)
            by_feature = lambda t: t.unsqueeze(1).to_broadcast(wide)
            sd = [0]

            def rooted():
                sd[0] += 1
                dve.wait_ge(s_sd, sd[0])

            def layernorm():
                link(v.tensor_reduce(st[:, 0, :], x[:], AX.X, ALU.add))
                link(v.tensor_scalar(st[:, 1, :], st[:, 0, :], -1.0 / D, None, ALU.mult))
                link(v.tensor_tensor(x[:], x[:], by_window(st[:, 1, :]), ALU.add))
                link(v.tensor_tensor(tmp, x[:], x[:], ALU.mult))
                link(v.tensor_reduce(st[:, 0, :], tmp, AX.X, ALU.add))
                v.tensor_scalar(st[:, 2, :], st[:, 0, :], 1.0 / D, EPS, ALU.mult, ALU.add).then_inc(s_sq, 1)
                rooted()
                link(v.reciprocal(st[:, 1, :], st[:, 3, :]))
                link(v.tensor_tensor(x[:], x[:], by_window(st[:, 1, :]), ALU.mult))

            plain_pass(pa0, WS, 0, 1)
            column = acc[:, :, ONE:ONE + 1].rearrange("p w a -> p (w a)")
            link(v.tensor_scalar(st[:, 0, :], column, 1.0, None, ALU.max))
            v.tensor_scalar(st[:, 2, :], column, 1.0, None, ALU.add).then_inc(s_sq, 1)
            link(v.reciprocal(st[:, 1, :], st[:, 0, :]))
            v.tensor_tensor(acc[:, :, 0:D], acc[:, :, 0:D], by_window(st[:, 1, :]), ALU.mult).then_inc(ready["l0_mean"], 1)
            rooted()
            link(v.reciprocal(dinv[:], st[:, 3, :]))
            project_dve(0, [tmp], dve)
            dve.wait_ge(s_pe, NW)
            dve.wait_ge(s_x, 32)
            link(v.tensor_tensor(x[:], x[:], tmp, ALU.add))
            layernorm()
            v.memset(acc, 0.0).then_inc(ready["l1_in"], 1)
            project_dve(1, [xr], dve)
            dve.wait_ge(s_pe, 2 * NW)
            v.tensor_tensor(xr[:], xr[:], by_window(dinv[:]), ALU.mult).then_inc(ready["l1_rows"], 1)
            dve.wait_ge(ready["l1_rows"], 1)
            plain_pass(pa1, WS, 0, 1)
            link(v.tensor_tensor(acc[:, :, 0:D], acc[:, :, 0:D], xr[:], ALU.add))
            link(v.tensor_tensor(acc[:, :, 0:D], acc[:, :, 0:D], by_window(dinv[:]), ALU.mult))
            link(v.tensor_tensor(x[:], x[:], acc[:, :, 0:D], ALU.add))
            layernorm()
            v.memset(st[:, 0, :], 0.0).then_inc(ready["l2_in"], 1)
            project_dve(2, [tmp, xr], dve)
            dve.wait_ge(s_pe, 3 * NW)
            v.tensor_tensor(zself, tmp, xr[:], ALU.add).then_inc(ready["l2_left"], 1)
            dve.wait_ge(ready["l2_left"], 1)
            link(v.scalar_tensor_tensor(zself, zself, 0.2, zself, ALU.mult, ALU.max))
            dve.wait_ge(s_vec, 16)
            link(v.tensor_tensor(zself, zself, by_feature(bc[:, 0, :]), ALU.mult))
            link(v.tensor_reduce(aself[:], big[:, 0:NW * D].rearrange("p (h c) -> p h c", c=C), AX.X, ALU.add))
            v.memset(rmax, LOW).then_inc(ready["l2_go"], 1)
            dve.wait_ge(ready["l2_go"], 1)

            def leaky(i, q):
                j = i * BODY + q
                dve.wait_ge(s_zc, j + 1)
                if later(i, q, BODY, 2):
                    dve.wait_ge(s_al, j - 1)
                v.scalar_tensor_tensor(lt[:, q % 2, :], zt[:, q % 2, :], 0.2, zt[:, q % 2, :], ALU.mult, ALU.max)\
                    .then_inc(s_lr, 1)

            def onehot_pen(i, q):
                j = i * BODY + q
                if q % 2 == 0:
                    dve.wait_ge(pa2.rec[q // 2], 16 * (i + 1))
                if later(i, q, BODY, BODY):
                    dve.wait_ge(s_rm, 2 * H * (j - BODY + 1))
                if later(i, q, BODY, 2):
                    dve.wait_ge(s_tr, j - 1)
                for u in range(2):
                    node = record(q // 2, 2 * (q % 2) + u, WD)[:, 1:2]
                    v.tensor_scalar(pen[:, q, u, :], iotab[:], node, LOW, ALU.not_equal, ALU.mult)
                    last = v.tensor_scalar(ohb[:, q % 2, u, :], iotab[:], node, None, ALU.is_equal)
                last.then_inc(pa2.oh, 1)

            def maxima_w(i, q, w):
                j = i * BODY + q
                dve.wait_ge(pa2.oh, j + 1)
                dve.wait_ge(s_alc, j + 1)
                for u in range(2):
                    for h in range(H):
                        if u or later(i, q, BODY, 1):
                            dve.wait_ge(s_rm, 2 * H * j + H * (u - 1) + h + 1)
                        r = row(rmax, w)[:, h * P:h * P + P]
                        v.scalar_tensor_tensor(r, pen[:, q, u, :], ps[:, 4 + q % 2, u * H + h:u * H + h + 1], r,
                                               ALU.add, ALU.max).then_inc(s_rm, 1)
            steps(dve, NP, BODY, [(0, onehot_pen), (2, leaky), (4, maxima_w)], (ET.DVE, bids[32:33, :], 4))

            def reduce(i, q):
                w = i * 2 + q
                dve.wait_ge(s_rt, w + 1)
                v.tensor_reduce(amax[:, bass.ds(w * H, H)], ps[:, q, :].rearrange("p (h e) -> p h e", h=H), AX.X, ALU.max)\
                    .then_inc(s_rr, 1)
            link(v.memset(amax[:], LOW))
            steps(dve, NB - 1, 2, [(0, reduce)])
            reduce(NB // 2, 0)
            dve.wait_ge(s_rr, NB)
            v.tensor_tensor(amax[:], amax[:], aself[:], ALU.max)
            v.memset(acc, 0.0).then_inc(ready["l2_sums"], 1)
            dve.wait_ge(ready["l2_sums"], 1)

            def shifted(i, q):
                j = i * BODY + q
                dve.wait_ge(b_sh, j + 1)
                if later(i, q, BODY, 2):
                    dve.wait_ge(b_exp, j - 1)
                v.tensor_tensor(ea8[:, q % 2, :], alpha[:, bass.ds(j, 1), :].rearrange("p a c -> p (a c)"),
                                ps[:, 4 + q % 2, 0:2 * H], ALU.subtract).then_inc(b_dif, 1)
                dve.wait_ge(b_dif, j + 1)
                v.tensor_scalar(ea8[:, q % 2, :], ea8[:, q % 2, :], 0.0, None, ALU.min).then_inc(b_sub, 1)

            def messages(i, q):
                j = i * BODY + q
                dve.wait_ge(b_exp, j + 1)
                dve.wait_ge(pb2.got[q % RING], 16 * (i * 2 + q // RING + 1))
                for u in range(2):
                    last = v.tensor_tensor(msg[:, q % 2, u, 0:D].rearrange("p (h c) -> p h c", h=H),
                                           g[:, q % RING, u, 0:D].rearrange("p (h c) -> p h c", h=H),
                                           msg[:, q % 2, u, D:AW].unsqueeze(2).to_broadcast([P, H, C]), ALU.mult)
                last.then_inc(b_msg, 1)
            steps(dve, NP, BODY, [(4, adds(pb2, AW)), (3, messages), (2, shifted),
                                  (0, onehots(pb2, WD, lambda n: dve.wait_ge(pb2.used, n)))], (ET.DVE, bids[32:33, :], 4))
            dve.wait_ge(pb2.acc, NP)
            v.tensor_tensor(eself, aself[:], amax[:], ALU.subtract).then_inc(ready["l2_sums_done"], 1)
            heads = lambda t: t.rearrange("p w (h c) -> p (w h) c", c=C)
            by_head = lambda t: t.unsqueeze(2).to_broadcast([P, NW * H, C])
            dve.wait_ge(s_exs, 1)
            dve.wait_ge(s_tab, 48)
            link(v.tensor_tensor(heads(tmp), heads(tmp), by_head(eself), ALU.mult))
            link(v.tensor_tensor(tmp, tmp, acc[:, :, 0:D], ALU.add))
            e3 = eself.rearrange("p (w h) -> p w h", h=H)
            link(v.tensor_tensor(e3, e3, acc[:, :, D:AW], ALU.add))
            link(v.tensor_scalar(eself, eself, 1e-16, None, ALU.add))
            link(v.reciprocal(eself, eself))
            link(v.tensor_tensor(heads(tmp), heads(tmp), by_head(eself), ALU.mult))
            dve.wait_ge(s_vec, 48)
            v.tensor_tensor(tmp, tmp, by_feature(bc[:, 0, :]), ALU.add).then_inc(ready["l2_conv_bias_used"], 1)
            dve.wait_ge(ready["l2_conv_bias_used"], 1)
            v.tensor_scalar(tmp, tmp, 0.0, None, ALU.max).then_inc(s_bng, 1)
            dve.wait_ge(s_bn, 1)
            mean, var, root = msg[:, 1, 0, 0:D], msg[:, 0, 0, 0:D], msg[:, 0, 1, 0:D]
            link(v.tensor_scalar(mean, ps[:, 4, 0:D], 1.0 / N, None, ALU.mult))
            link(v.tensor_tensor(tmp, tmp, by_feature(mean), ALU.subtract))
            v.tensor_tensor(xr[:], tmp, tmp, ALU.mult).then_inc(s_bng, 1)
            dve.wait_ge(s_bn, 2)
            v.tensor_scalar(var, ps[:, 5, 0:D], 1.0 / N, EPS, ALU.mult, ALU.add).then_inc(s_sq, 1)
            rooted()
            link(v.reciprocal(var, root))
            link(v.tensor_tensor(var, var, bc[:, 1, :], ALU.mult))
            link(v.tensor_tensor(tmp, tmp, by_feature(var), ALU.mult))
            dve.wait_ge(s_vec, 64)
            v.tensor_tensor(tmp, tmp, by_feature(bc[:, 0, :]), ALU.add).then_inc(ready["l2_norm"], 1)
            project_dve(3, [xr], dve)
            dve.wait_ge(s_pe, 4 * NW)
            link(v.tensor_tensor(x[:], x[:], xr[:], ALU.add))
            layernorm()
            v.memset(acc, 0.0)
            v.memset(msg[:, :, :, ONE:ONE + 1], 1.0).then_inc(ready["l3_in"], 1)
            project_dve(4, [xr], dve)
            dve.wait_ge(s_pe, 5 * NW)
            dve.wait_ge(ready["l3_in"], 1)
            v.memset(st[:, 0, :], 0.0).then_inc(ready["l3_rows"], 1)
            plain_pass(pa3, WD, 1, 3)
            v.memset(st[:, 0, :], 0.0).then_inc(ready["l3_sums"], 1)
            project_dve(5, [tmp], dve)
            dve.wait_ge(s_pe, 6 * NW)
            dve.wait_ge(s_vec, 96)
            link(v.tensor_copy(st[:, 1, :], column))
            link(v.tensor_copy(zself, x[:]))
            v.tensor_tensor(x[:], x[:], tmp, ALU.add)
            link(v.tensor_tensor(xr[:], by_window(st[:, 1, :]), by_feature(bc[:, 0, :]), ALU.mult))
            v.tensor_tensor(x[:], x[:], xr[:], ALU.add).then_inc(ready["l3_b2_used"], 1)
            dve.wait_ge(ready["l3_b2_used"], 1)
            layernorm()
            link(v.tensor_tensor(x[:], x[:], by_feature(bc[:, 1, :]), ALU.mult))
            dve.wait_ge(s_vec, 112)
            link(v.tensor_tensor(x[:], x[:], by_feature(bc[:, 0, :]), ALU.add))
            link(v.tensor_tensor(x[:], x[:], zself, ALU.add))
            layernorm()
            v.memset(st[:, 0, :], 0.0).then_inc(ready["out"], 1)


_INS = ["x", "src", "dst", "edge_attr_3", "L0_gnn_x_clique", "L0_gnn_W", "L0_gnn_b", "L1_gnn_W", "L1_gnn_b",
        "L2_gnn_lin_l_w", "L2_gnn_lin_l_b", "L2_gnn_lin_r_w", "L2_gnn_lin_r_b", "L2_gnn_att", "L2_gnn_conv_bias",
        "L2_gnn_lin_w", "L2_gnn_lin_b", "L2_gnn_bn_gamma", "L2_gnn_bn_beta", "L3_gnn_W1", "L3_gnn_b1", "L3_gnn_W2",
        "L3_gnn_b2", "L3_gnn_gamma", "L3_gnn_beta"]


def kernel(**inputs):
    import numpy as _np
    import concourse.bacc as _bacc
    from concourse import mybir as _mybir
    from concourse.bass_utils import run_bass_kernel_spmd as _run

    nc = _bacc.Bacc("TRN2", target_bir_lowering=False, num_devices=1)
    arrays, args = {}, {}
    for name in _INS:
        arr = _np.ascontiguousarray(inputs[name])
        arrays[f"in_{name}"] = arr
        args[name] = nc.dram_tensor(f"in_{name}", arr.shape, _mybir.dt.from_np(arr.dtype), kind="ExternalInput").ap()
    out = nc.dram_tensor("out_0", (N, D), F32, kind="ExternalOutput").ap()
    gnn_kernel(nc, args, out)
    r = _run(nc, [arrays], core_ids=[0])
    return r.results[0]["out_0"]
```

```python
from contextlib import ExitStack

import concourse.bass as bass
from concourse import mybir

F32 = mybir.dt.float32
I32 = mybir.dt.int32
BF16 = mybir.dt.bfloat16
ALU = mybir.AluOpType
ACT = mybir.ActivationFunctionType
AX = mybir.AxisListType
ET = mybir.EngineType

P = 128
D = 128
N = 6250
E = 200000
H, C = 4, 32
FULL = N // P
REST = N - FULL * P
NB = 49
NW = NB + 1
NC = 1568
LASTC = E - (P - 1) * NC
PADNODE = NB * P - 1
PAIR = 2 * P
GROUP = 8
BODY = 16
NP = -(-((P * NC + NB * (PAIR - 1)) // PAIR) // BODY) * BODY
T = 2 * NP
WS, WD = 4, 8
AW = D + H
ONE = D
EPS = 1e-5
LOW = -1e30
RING = 4
FILLERS = 8
PARTS = 4
CONSTS = 9
FILLS = 6
BIG = max(NB * H * P, NW * AW + NC * (WS + WD))


def gnn_kernel(nc, a, out):
    with ExitStack() as ctx:
        def sb(name, shape, dt=F32):
            return ctx.enter_context(nc.sbuf_tensor(name, shape, dt))

        def sem(name):
            return ctx.enter_context(nc.semaphore(name))

        recs_dram = nc.dram_tensor("recs_dram", [P, T, WS], F32).ap()
        recd_dram = nc.dram_tensor("recd_dram", [P, T, WD], F32).ap()
        tab1 = nc.dram_tensor("tab1", [NW * P, D], F32).ap()
        tab2 = nc.dram_tensor("tab2", [NW * P, D], F32).ap()
        tab3 = nc.dram_tensor("tab3", [NW * P, D], F32).ap()
        lin_dram = nc.dram_tensor("lin_dram", [P * NC + PAIR, WD], F32).ap()
        rows2 = nc.dram_tensor("rows2", [P, NP, 2 * D], F32).ap()

        x = sb("x", [P, NW, D])
        xr = sb("xr", [P, NW, D])
        big = sb("big", [P, BIG])
        alp = sb("alp", [P, T * H])
        acc = big[:, 0:NW * AW].rearrange("p (w f) -> p w f", w=NW)
        zself = big[:, 0:NW * D].rearrange("p (w f) -> p w f", w=NW)
        rmax = big[:, 0:NB * H * P].rearrange("p (w f) -> p w f", w=NB)
        tmp = alp[:, 0:NW * D].rearrange("p (w f) -> p w f", w=NW)
        alpha = alp[:].rearrange("p (j c) -> p j c", j=NP)
        eself = big[:, NW * AW:NW * AW + NW * H]
        o = NW * AW
        recd = big[:, o:o + NC * WD].rearrange("p (c w) -> p c w", w=WD)
        recs = big[:, o + NC * WD:o + NC * (WD + WS)].rearrange("p (c w) -> p c w", w=WS)
        srci = alp[:, 0:NC].bitcast(I32)
        dsti = alp[:, NC:2 * NC].bitcast(I32)
        mask = alp[:, 2 * NC:3 * NC]
        scan = alp[:, 3 * NC:4 * NC]
        xflat = x[:].rearrange("p w f -> p (w f)")
        xrflat = xr[:].rearrange("p w f -> p (w f)")
        FT = T // FILLERS
        filld = xflat[:, 0:FT * WD].rearrange("p (t w) -> p t w", w=WD)
        fills = xflat[:, FT * WD:FT * (WD + WS)].rearrange("p (t w) -> p t w", w=WS)
        o = FT * (WD + WS)
        key = xflat[:, o:o + NC]
        pos = xflat[:, o + NC:o + 2 * NC]
        ea = xrflat[:, 0:3 * NC]
        wraw = xrflat[:, 3 * NC:3 * NC + 4 * D].rearrange("p (k f) -> p k f", k=4)
        iotap = xrflat[:, 3 * NC + 4 * D:3 * NC + 4 * D + NP]
        ltri = xrflat[:, 3 * NC + 4 * D + NP:3 * NC + 4 * D + NP + P]

        base = xrflat[:, 0:NP]
        fix = xrflat[:, NP:NP + 2 * 8 * WD].rearrange("p (h t w) -> p h t w", h=2, t=8)
        nexti = sb("nexti", [P, 1], I32)
        unsorted = sb("unsorted", [1, 1], I32)
        ident = sb("ident", [P, P])
        ones = sb("ones", [P, P])
        iota = sb("iota", [P, P])
        iotab = sb("iotab", [P, P], BF16)
        identb = sb("identb", [P, P], BF16)
        bids = sb("bids", [97, NP], I32)
        rows = bids[64:65, 0:3 * D].bitcast(F32)
        rec = sb("rec", [P, 4, 4, WD])
        recs4 = rec[:].rearrange("p k t (a w) -> p (k t a) w", a=2)
        g = sb("g", [P, RING, 2, AW])
        oh = sb("oh", [P, RING, 2, P])
        pen = oh[:].rearrange("p a u d -> p (a u d)").bitcast(BF16).rearrange("p (a u d) -> p a u d", a=GROUP, u=2)
        oht = sb("oht", [P, 2, PAIR])
        zt = sb("zt", [P, 2, PAIR])
        msg = sb("msg", [P, 2, 2, AW])
        xb = sb("xb", [P, 2, D])
        w01 = sb("w01", [P, 2 * D])
        w0t, w1 = w01[:, 0:D], w01[:, D:2 * D]
        ohb = w01[:].bitcast(BF16).rearrange("p (a u d) -> p a u d", a=2, u=2)
        wlrt = sb("wlrt", [P, 2 * D])
        lint = sb("lint", [P, D])
        w31 = sb("w31", [P, D])
        w32 = sb("w32", [P, D])
        w31b = sb("w31b", [2 * WD, 2, D])
        attm = sb("attm", [P, H])
        bc = sb("bc", [P, 2, D])
        cnt = sb("cnt", [P, NW])
        dinv = sb("dinv", [P, NW])
        st = sb("st", [P, 4, NW])
        aself = sb("aself", [P, NW * H])
        amax = sb("amax", [P, NW * H])
        ea8 = sb("ea8", [P, 2, 2 * H])
        amax3 = zt[:].rearrange("p a e -> p (a e)").bitcast(BF16)[:, 0:3 * NW * H].rearrange("p (w k h) -> p w k h", w=NW, k=3)
        lt = msg[:].rearrange("p a u f -> p (a u f)")[:, 0:2 * PAIR].rearrange("p (a e) -> p a e", a=2)
        rfix = g[:].rearrange("p a u f -> p (a u f)")[:, 0:2 * H * P].rearrange("p (a f) -> p a f", a=2)

        ps = ctx.enter_context(nc.psum_tensor("ps", [P, 8, 512], F32))

        ntab = lambda t: t.rearrange("(w p) f -> p w f", p=P)

        s_const = sem("const_made")
        s_load = sem("weights_in")
        s_edges = sem("edges_in")
        s_fill = sem("fill_made")
        s_filled = sem("records_filled")
        s_pad = sem("pad_made")
        s_ea = sem("attributes_in")
        s_eac = sem("attributes_placed")
        s_wt = sem("weight_transposed")
        s_wtc = sem("weight_copied")
        s_v = sem("vector_chain")
        s_cnt = sem("window_counts")
        s_pre = sem("window_prefixes")
        s_cum = sem("window_starts")
        s_cmp = sem("pair_windows_compared")
        s_cmpd = sem("pair_windows_summed")
        s_rank = [sem(f"{o}_rows_ranked") for o in ("src", "dst")]
        s_stage = [[sem(f"{o}_staged{h}") for h in range(2)] for o in ("src", "dst")]
        s_scat = [[sem(f"{o}_scattered{h}") for h in range(2)] for o in ("src", "dst")]
        s_filled_dst = sem("dst_records_filled")
        s_count = sem("unsorted_counted")
        s_first = sem("first_edges_known")
        s_empty = sem("empty_records_made")
        s_lin = sem("linear_records_stored")
        s_run = [sem(f"runs_in{h}") for h in range(2)]
        s_node = sem("run_nodes_made")
        s_runout = [sem(f"runs_stored{h}") for h in range(2)]
        s_dst = sem("dst_records_ready")
        s_vg = sem("general_vector_chain")
        s_x = sem("x_in")
        s_pc, s_pt, s_pa, s_pm, s_pe = (sem(f"project_{n}") for n in ("copied", "turned", "turned_copied", "product", "out"))
        ready = {n: sem(f"ready_{n}") for n in (
            "x_zero", "l0_mean", "l1_in", "l1_rows", "l2_in", "l2_left", "l2_go", "l2_sums", "l2_sums_done",
            "l2_conv_bias_used", "l2_norm", "l3_in", "l3_rows", "l3_sums", "l3_b2_used", "out")}
        s_sq = sem("squares_ready")
        s_sd = sem("roots_ready")
        s_tab = sem("table_stored")
        s_vec = sem("vectors_in")
        s_bn = sem("batch_sums")
        s_done = sem("out_stored")
        s_cmpr = sem("pair_windows_kept")
        b_dif = sem("l2b_difference_clamped")
        s_clear = sem("pool_cleared")
        s_exs = sem("self_weights_made")
        s_rc, s_rt, s_rr = sem("max_copied"), sem("max_turned"), sem("max_reduced")
        s_bng = sem("batch_operand_ready")

        class Pass:
            def __init__(self, name):
                self.rec = [sem(f"{name}_records_in{k}") for k in range(4)]
                self.got = [sem(f"{name}_rows_in{k}") for k in range(RING)]
                self.oh = sem(f"{name}_onehot_made")
                self.used = sem(f"{name}_rows_used")
                self.acc = sem(f"{name}_sums_added")

        pa0, pa1, pa2, pb2, pa3 = (Pass(n) for n in ("l0", "l1", "l2a", "l2b", "l3"))
        s_kept = [sem(f"l2a_rows_kept{k}") for k in range(RING)]
        s_tr = sem("l2a_onehot_turned")
        s_trc = sem("l2a_onehot_turned_copied")
        s_pen = sem("l2a_penalties_made")
        s_zc = sem("l2a_sum_copied")
        s_lr = sem("l2a_leaky_made")
        s_al = sem("l2a_logits_made")
        s_alc = sem("l2a_logits_kept")
        s_rm = sem("l2a_max_updated")
        b_tr = sem("l2b_onehot_turned")
        b_trc = sem("l2b_onehot_turned_copied")
        b_sh = sem("l2b_shift_made")
        b_sub = sem("l2b_logits_shifted")
        b_exp = sem("l2b_weights_made")
        b_msg = sem("l2b_messages_made")
        c_tr = sem("l3_records_turned")
        c_trc = sem("l3_records_turned_copied")
        c_z = sem("l3_hidden_made")
        c_msg = sem("l3_gelu_made")

        def steps(eng, n, unroll, stages, regs=None):
            def load(first, count, lag_reg=None):
                e, bid_row = regs[0], regs[1]
                return nc.values_load_multi_w_load_instructions(
                    bid_row[:, first] if isinstance(first, slice) else bid_row[:, bass.ds(first, count)],
                    engines=[e], min_val=0, max_val=NB - 1,
                    skip_runtime_bounds_check_because="a pair's window is clamped to the last one")[1]
            most = max(lag for lag, _ in stages)
            rlag = regs[2] if regs else 0

            def call(f, i, q, w):
                f(i, q) if w is None else f(i, q, w)

            w = load(0, unroll - rlag) if regs else None
            for q in range(unroll):
                for lag, f in stages:
                    if q >= lag:
                        call(f, 0, q - lag, w[q - lag] if regs and lag == rlag and f.__name__.endswith("_w") else None)
            with eng.Fori(1, n // unroll) as i:
                w = load(i * unroll - rlag, unroll) if regs else None
                for q in range(unroll):
                    for lag, f in stages:
                        call(f, i if q >= lag else i - 1, (q - lag) % unroll,
                             w[q] if regs and f.__name__.endswith("_w") else None)
            if most:
                w = load(n - rlag, rlag) if regs and rlag else None
                for q in range(most):
                    for lag, f in stages:
                        if lag > q:
                            call(f, n // unroll - 1, unroll + q - lag, w[q] if regs and f.__name__.endswith("_w") else None)

        def later(i, q, unroll, r):
            return not isinstance(i, int) or i * unroll + q >= r

        def turn(i, q, ring):
            return i * (BODY // ring) + q // ring

        def quad(q):
            return q // 2 % 4

        def row(t, w):
            return t[:, bass.ds(w, 1), :].rearrange("p a f -> p (a f)")

        def is_unsorted(eng, e):
            eng.wait_ge(s_count, 1)
            return nc.values_load_multi_w_load_instructions(
                unsorted[0:1, 0:1], engines=[e], min_val=0, max_val=P * NC,
                skip_runtime_bounds_check_because="it counts edges")[1][0]

        block = ctx.enter_context(nc.Block())


        def project_act(k, src, act):
            base = NW * k

            def fix(i, q):
                w = i * 2 + q
                if k or later(i, q, 2, 2):
                    act.wait_ge(s_pt, base + w - 1)
                nc.scalar.activation(xb[:, q, :], row(src, w), ACT.Copy).then_inc(s_pc, 1)

            def turned(i, q):
                w = i * 2 + q
                act.wait_ge(s_pt, base + w + 1)
                if k or later(i, q, 2, 2):
                    act.wait_ge(s_pm, base + w - 1)
                nc.scalar.activation(zt[:, q, 0:P], ps[:, q, 0:P], ACT.Copy).then_inc(s_pa, 1)
            steps(act, NW, 2, [(0, fix), (1, turned)])

        def project_pe(k, wt, m, b, pe):
            base = NW * k

            def turn_w(i, q):
                w = i * 2 + q
                pe.wait_ge(s_pc, base + w + 1)
                if k or later(i, q, 2, 2):
                    pe.wait_ge(s_pa, base + w - 1)
                nc.tensor.transpose(ps[:, q, 0:P], xb[:, q, :], ident[:]).then_inc(s_pt, 1)

            def product(i, q):
                w = i * 2 + q
                pe.wait_ge(s_pa, base + w + 1)
                if k or later(i, q, 2, 2):
                    pe.wait_ge(s_pe, base + w - 1)
                last = nc.tensor.matmul(ps[:, 2 + q, 0:m], zt[:, q, 0:P], wt[:, 0:m], start=True, stop=b is None)
                if b is not None:
                    last = nc.tensor.matmul(ps[:, 2 + q, 0:m], ones[64:65, :], rows[:, b * D:b * D + m], start=False, stop=True)
                last.then_inc(s_pm, 1)
            steps(pe, NW, 2, [(0, turn_w), (1, product)])

        def project_dve(k, dsts, dve, scale=None, add=False, bias=None):
            base = NW * k

            def leave(i, q):
                w = i * 2 + q
                dve.wait_ge(s_pm, base + w + 1)
                for n, dst in enumerate(dsts):
                    result = ps[:, 2 + q, n * D:n * D + D]
                    if scale is not None:
                        last = nc.vector.tensor_scalar(row(dst, w), result, scale[:, bass.ds(w, 1)], None, ALU.mult)
                    elif bias is not None:
                        last = nc.vector.tensor_tensor(row(dst, w), result, bias[:, n, :], ALU.add)
                    elif add:
                        last = nc.vector.tensor_tensor(row(dst, w), row(dst, w), result, ALU.add)
                    else:
                        last = nc.vector.tensor_copy(row(dst, w), result)
                last.then_inc(s_pe, 1)
            steps(dve, NW, 2, [(0, leave)])

        def record(k, t, words):
            return rec[:, k, t, :] if words == WD else rec[:, k, t // 2, WS * (t % 2):WS * (t % 2) + WS]

        def records(k, words):
            return rec[:, k, :, :] if words == WD else rec[:, k, 0:2, :].rearrange("p t (a w) -> p (t a) w", a=2)

        @block.sync
        def _(sp):
            sp.wait_ge(s_pad, 3)
            sp.dma_start(nexti[0:P - 2, :], a["dst"][NC:(P - 1) * NC].rearrange("(p c) -> p c", c=NC)[:, 0:1],
                         allow_slow_non_contiguous=True).then_inc(s_edges, 16)
            sp.dma_start(nexti[P - 2:P - 1, :],
                         a["dst"][(P - 1) * NC:(P - 1) * NC + 1].rearrange("(p c) -> p c", p=1)).then_inc(s_edges, 16)
            for t, name in ((srci, "src"), (dsti, "dst")):
                v = a[name][0:(P - 1) * NC].rearrange("(p c) -> p c", c=NC)
                sp.dma_start(t[0:112, :], v[0:112, :]).then_inc(s_edges, 16)
                sp.dma_start(t[112:P - 1, :], v[112:P - 1, :]).then_inc(s_edges, 16)
                sp.dma_start(t[P - 1:P, 0:LASTC],
                             a[name][(P - 1) * NC:E].rearrange("(p c) -> p c", p=1)).then_inc(s_edges, 16)
            v = a["edge_attr_3"][0:(P - 1) * NC, :].rearrange("(p c) k -> p (c k)", c=NC)
            sp.dma_start(ea[0:112, :], v[0:112, :]).then_inc(s_ea, 16)
            sp.dma_start(ea[112:P - 1, :], v[112:P - 1, :]).then_inc(s_ea, 16)
            sp.dma_start(ea[P - 1:P, 0:3 * LASTC],
                         a["edge_attr_3"][(P - 1) * NC:E, :].rearrange("(p c) k -> p (c k)", p=1)).then_inc(s_ea, 16)
            for dst, src in ((wraw[:, 0, :], a["L0_gnn_W"]), (wraw[:, 1, :], a["L2_gnn_lin_l_w"]),
                             (wraw[:, 2, :], a["L2_gnn_lin_r_w"]), (wraw[:, 3, :], a["L2_gnn_lin_w"]),
                             (w1, a["L1_gnn_W"]), (w31[:], a["L3_gnn_W1"][0:D, :]), (w32[:], a["L3_gnn_W2"])):
                sp.dma_start(dst, src).then_inc(s_load, 16)
            sp.dma_start(bc[:, 0, :], a["L0_gnn_b"].partition_broadcast(P)).then_inc(s_vec, 16)
            for n, name in enumerate(("L1_gnn_b", "L2_gnn_lin_b", "L3_gnn_b1")):
                sp.dma_start(rows[:, n * D:n * D + D], a[name].rearrange("(p f) -> p f", p=1)).then_inc(s_load, 16)
            sp.wait_ge(s_const, CONSTS)
            for u in range(2):
                sp.dma_start(w31b[u * WD + 2:u * WD + 5, u, :], a["L3_gnn_W1"][D:D + 3, :]).then_inc(s_load, 16)
            for h in range(H):
                sp.dma_start(attm[C * h:C * h + C, h:h + 1],
                             a["L2_gnn_att"][0, h, :].rearrange("(c b) -> c b", b=1)).then_inc(s_load, 16)
            sp.wait_ge(s_fill, FILLS)
            for k in range(FILLERS):
                sp.dma_start(recs_dram[:, k * FT:k * FT + FT, :], fills).then_inc(s_filled, 16)

            def stage(order, src, words):
                for part in range(PARTS):
                    sp.wait_ge(s_rank[order], part + 1)

                    def move(i, h):
                        i = i + part * (NC // 8 // PARTS)
                        if part or later(i, h, 2, 2):
                            sp.wait_ge(s_scat[order][h], 64 * i)
                        sp.dma_start(records(h, words), src[:, bass.ds(i * 8 + 4 * h, 4), :]).then_inc(s_stage[order][h], 16)
                    steps(sp, NC // 4 // PARTS, 2, [(0, move)])
            stage(0, recs, WS)
            for h in range(2):
                sp.wait_ge(s_scat[0][h], 64 * NC // 8)
            with sp.If(is_unsorted(sp, ET.SP) > 0):
                for k in range(FILLERS):
                    sp.dma_start(recd_dram[:, k * FT:k * FT + FT, :], filld).then_inc(s_filled_dst, 16)
                sp.wait_ge(s_eac, 3)
                stage(1, recd, WD)
                for h in range(2):
                    sp.wait_ge(s_scat[1][h], 64 * NC // 8)
            sp.wait_ge(ready["x_zero"], 1)
            sp.dma_start(x[:, 0:FULL, :], a["x"][0:FULL * P, :].rearrange("(w p) f -> p w f", p=P)).then_inc(s_x, 16)
            sp.dma_start(x[0:REST, FULL, :], a["x"][FULL * P:N, :]).then_inc(s_x, 16)
            def stream(pas, dram, words):
                def load(i, k):
                    sp.dma_start(records(k, words), dram[:, bass.ds((i * GROUP + 2 * k) * 2, 4), :]).then_inc(pas.rec[k], 16)
                for k in range(4):
                    load(0, k)
                with sp.Fori(1, NP // GROUP) as i:
                    for k in range(4):
                        sp.wait_ge(pas.used, i * GROUP + 2 * k + 2 - GROUP)
                        load(i, k)
            stream(pa0, recs_dram, WS)
            sp.wait_ge(ready["l1_rows"], 1)
            sp.dma_start(ntab(tab1), xr[:]).then_inc(s_tab, 16)
            for n, name in enumerate(("L2_gnn_lin_l_b", "L2_gnn_lin_r_b")):
                sp.dma_start(bc[:, n, :], a[name].partition_broadcast(P)).then_inc(s_vec, 16)
            stream(pa1, recs_dram, WS)
            sp.wait_ge(ready["l2_left"], 1)
            sp.dma_start(ntab(tab2), tmp).then_inc(s_tab, 16)
            sp.dma_start(bc[:, 0, :], a["L2_gnn_att"].rearrange("a h c -> (a h c)").partition_broadcast(P)).then_inc(s_vec, 16)

            def load2(pas, i, k):
                sp.dma_start(records(k, WD), recd_dram[:, bass.ds((i * GROUP + 2 * k) * 2, 4), :]).then_inc(pas.rec[k], 16)

            def keep(i, q):
                s = q % RING
                sp.wait_ge(pa2.got[s], 32 * (i * 2 + q // RING + 1))
                sp.dma_start(rows2[:, bass.ds(i * GROUP + q, 1), :].rearrange("p a (t f) -> p (a t) f", t=2),
                             g[:, s, :, 0:D]).then_inc(s_kept[s], 16)

            def reload(i, q):
                sp.wait_ge(pa2.oh, i * GROUP + q + 1)
                load2(pa2, i + 1, q // 2)
            sp.wait_ge(s_dst, 1)
            for k in range(4):
                load2(pa2, 0, k)
            last = NP // GROUP - 1
            for q in range(GROUP):
                keep(0, q)
                if q in (3, 5, 7):
                    reload(0, q - 2)
            with sp.Fori(1, last) as i:
                for q in range(GROUP):
                    keep(i, q)
                    if q == 1:
                        reload(i - 1, GROUP - 1)
                    elif q % 2 == 1:
                        reload(i, q - 2)
            for q in range(GROUP):
                keep(last, q)
                if q == 1:
                    reload(last - 1, GROUP - 1)
            for s in range(RING):
                sp.wait_ge(s_kept[s], 16 * NP // RING)

            sp.wait_ge(ready["l2_sums"], 1)

            def again(i, q):
                s = q % RING
                if q % 2 == 0:
                    if later(i, q, GROUP, GROUP):
                        sp.wait_ge(pb2.oh, i * GROUP + q + 2 - GROUP)
                    load2(pb2, i, q // 2)
                if later(i, q, GROUP, RING):
                    sp.wait_ge(b_msg, i * GROUP + q - RING + 1)
                sp.dma_start(g[:, s, :, 0:D], rows2[:, bass.ds(i * GROUP + q, 1), :].rearrange("p a (t f) -> p (a t) f", t=2))\
                    .then_inc(pb2.got[s], 16)
            steps(sp, NP, GROUP, [(0, again)])
            sp.wait_ge(ready["l2_sums_done"], 1)
            sp.dma_start(tmp, ntab(tab2)).then_inc(s_tab, 16)
            for n, name in enumerate(("L2_gnn_conv_bias", "L2_gnn_bn_gamma")):
                sp.dma_start(bc[:, n, :], a[name].partition_broadcast(P)).then_inc(s_vec, 16)
            sp.wait_ge(ready["l2_conv_bias_used"], 1)
            sp.dma_start(bc[:, 0, :], a["L2_gnn_bn_beta"].partition_broadcast(P)).then_inc(s_vec, 16)
            sp.wait_ge(ready["l3_rows"], 1)
            sp.dma_start(ntab(tab3), xr[:]).then_inc(s_tab, 16)
            sp.dma_start(bc[:, 0, :], a["L3_gnn_b2"].partition_broadcast(P)).then_inc(s_vec, 16)
            sp.dma_start(bc[:, 1, :], a["L3_gnn_gamma"].partition_broadcast(P)).then_inc(s_vec, 16)
            stream(pa3, recd_dram, WD)
            sp.wait_ge(ready["l3_b2_used"], 1)
            sp.dma_start(bc[:, 0, :], a["L3_gnn_beta"].partition_broadcast(P)).then_inc(s_vec, 16)
            sp.wait_ge(ready["out"], 1)
            sp.dma_start(out[0:FULL * P, :].rearrange("(w p) f -> p w f", p=P), x[:, 0:FULL, :]).then_inc(s_done, 16)
            sp.dma_start(out[FULL * P:N, :], x[0:REST, FULL, :]).then_inc(s_done, 16)
            sp.wait_ge(s_done, 32)

        @block.gpsimd
        def _(pool):
            gp = nc.gpsimd
            gp.memset(srci, PADNODE).then_inc(s_pad, 1)
            gp.memset(dsti, PADNODE).then_inc(s_pad, 1)
            gp.memset(nexti[:], PADNODE).then_inc(s_pad, 1)
            gp.memset(recs, 0.0).then_inc(s_fill, 1)
            gp.memset(recd, 0.0).then_inc(s_fill, 1)
            gp.memset(filld, 0.0).then_inc(s_fill, 1)
            gp.memset(fills, 0.0).then_inc(s_fill, 1)
            pool.wait_ge(s_fill, 4)
            gp.memset(filld[:, :, 1:2], -1.0).then_inc(s_fill, 1)
            gp.memset(fills[:, :, 1:2], -1.0).then_inc(s_fill, 1)
            gp.memset(ident[:], 0.0).then_inc(s_const, 1)
            gp.memset(ones[:], 1.0).then_inc(s_const, 1)
            gp.iota(iota[:], [[1, P]], base=0, channel_multiplier=0, allow_small_or_imprecise_dtypes=True).then_inc(s_const, 1)
            gp.memset(w31b[:], 0.0).then_inc(s_const, 1)
            gp.memset(attm[:], 0.0).then_inc(s_const, 1)
            gp.memset(g[:, :, :, ONE:ONE + 1], 1.0).then_inc(s_const, 1)
            gp.iota(iotap, [[1, NP]], base=0, channel_multiplier=0, allow_small_or_imprecise_dtypes=True).then_inc(s_const, 1)
            pool.wait_ge(s_const, CONSTS - 2)
            gp.affine_select(out=ident[:], in_=ident[:], compare_op=ALU.not_equal, fill=1.0, base=0,
                             pattern=[[-1, P]], channel_multiplier=1).then_inc(s_const, 1)
            gp.affine_select(out=ltri, in_=ones[:], compare_op=ALU.is_gt, fill=0.0, base=0,
                             pattern=[[1, P]], channel_multiplier=-1).then_inc(s_const, 1)

            def scatter(order, words, dram):
                table = dram.rearrange("p t w -> (p t) w")

                def tiles(i, h):
                    pool.wait_ge(s_stage[order][h], 16 * (i + 1))
                    pool.sem_inc(s_clear, 1)
                    for t in range(4):
                        r = record(h, t, words)
                        gp.indirect_dma_start(
                            out=table, out_offset=bass.IndirectOffsetOnAxis(ap=r[:, words - 1:words].bitcast(I32), axis=0),
                            in_=r, in_offset=None).then_inc(s_scat[order][h], 16)
                steps(pool, NC // 4, 2, [(0, tiles)])

            def gathers(pas, words, table, kept=None):
                def pair(i, q):
                    s, k = q % RING, quad(q)
                    if q % 2 == 0:
                        pool.wait_ge(pas.rec[k], 16 * (turn(i, q, GROUP) + 1))
                    if later(i, q, BODY, RING):
                        pool.wait_ge(pas.used, i * BODY + q - RING + 1)
                        if kept is not None:
                            pool.wait_ge(kept[s], 16 * (turn(i, q, RING)))
                    pool.sem_inc(s_clear, 1)
                    for u in range(2):
                        gp.indirect_dma_start(
                            out=g[:, s, u, 0:D], out_offset=None, in_=table,
                            in_offset=bass.IndirectOffsetOnAxis(
                                ap=record(k, 2 * (q % 2) + u, words)[:, 0:1].bitcast(I32), axis=0)).then_inc(pas.got[s], 16)
                steps(pool, NP, BODY, [(0, pair)])

            pool.wait_ge(s_filled, 16 * FILLERS)
            scatter(0, WS, recs_dram)
            with pool.If(is_unsorted(pool, ET.Pool) > 0):
                pool.wait_ge(s_filled_dst, 16 * FILLERS)
                scatter(1, WD, recd_dram)
                for h in range(2):
                    pool.wait_ge(s_scat[1][h], 64 * NC // 8)
                pool.sem_inc(s_dst, 1)
            gathers(pa0, WS, a["L0_gnn_x_clique"])
            pool.wait_ge(s_tab, 16)
            gathers(pa1, WS, tab1)
            pool.wait_ge(s_tab, 32)
            gathers(pa2, WD, tab2, s_kept)
            pool.wait_ge(s_tab, 64)
            gathers(pa3, WD, tab3)

        @block.scalar
        def _(act):
            sc = nc.scalar
            act.wait_ge(s_ea, 48)
            act.wait_ge(s_fill, 4)
            ea3 = ea.rearrange("p (c k) -> p c k", k=3)
            sc.activation(recd[0:96, :, 2:5], ea3[0:96], ACT.Copy).then_inc(s_eac, 1)
            sc.activation(recd[96:P, 0:LASTC, 2:5], ea3[96:P, 0:LASTC], ACT.Copy).then_inc(s_eac, 1)
            sc.activation(recd[96:P - 1, LASTC:NC, 2:5], ea3[96:P - 1, LASTC:NC], ACT.Copy).then_inc(s_eac, 1)
            for k, dst in enumerate((w0t, wlrt[:, 0:D], wlrt[:, D:2 * D], lint[:])):
                act.wait_ge(s_wt, k + 1)
                sc.activation(dst, ps[:, k, 0:P], ACT.Copy).then_inc(s_wtc, 1)

            act.wait_ge(s_first, 1)
            with act.If(is_unsorted(act, ET.Activation) < 1):
                act.wait_ge(s_eac, 3)
                act.dma_start(lin_dram[0:P * NC, :].rearrange("(p c) w -> p (c w)", c=NC),
                              recd.rearrange("p c w -> p (c w)")).then_inc(s_lin, 16)
                act.wait_ge(s_empty, 3)
                act.dma_start(lin_dram[P * NC:P * NC + PAIR, :].rearrange("(p c) w -> p (c w)", c=2),
                              fix[:, 0, 0:2, :].rearrange("p c w -> p (c w)")).then_inc(s_lin, 16)
                act.wait_ge(s_lin, 32)

                def runs(i, first):
                    e = nc.values_load_multi_w_load_instructions(
                        bids[96:97, bass.ds(i * 8, 8)] if not first else bids[96:97, 0:8],
                        engines=[ET.Activation], min_val=0, max_val=P * NC,
                        skip_runtime_bounds_check_because="it is clamped to the empty records")[1]
                    for h in range(2):
                        if not first:
                            act.wait_ge(s_runout[h], 16 * i)
                        for k in range(4):
                            act.dma_start(fix[:, h, 2 * k:2 * k + 2, :].rearrange("p c w -> p (c w)"),
                                          lin_dram[bass.ds(e[4 * h + k], PAIR), :].rearrange("(p c) w -> p (c w)", c=2))\
                                .then_inc(s_run[h], 16)
                    for h in range(2):
                        act.wait_ge(s_node, i * 2 + h + 1)
                        act.dma_start(recd_dram[:, bass.ds(i * 16 + 8 * h, 8), :], fix[:, h, :, :]).then_inc(s_runout[h], 16)
                runs(0, True)
                with act.Fori(1, NP // 8) as i:
                    runs(i, False)
                for h in range(2):
                    act.wait_ge(s_runout[h], 16 * NP // 8)
                act.sem_inc(s_dst, 1)

            def roots(n):
                act.wait_ge(s_sq, n + 1)
                sc.activation(st[:, 3, :], st[:, 2, :], ACT.Sqrt).then_inc(s_sd, 1)

            roots(0)
            act.wait_ge(ready["l0_mean"], 1)
            project_act(0, acc[:, :, 0:D], act)
            roots(1)
            act.wait_ge(ready["l1_in"], 1)
            project_act(1, x, act)
            roots(2)
            act.wait_ge(ready["l2_in"], 1)
            project_act(2, x, act)

            act.wait_ge(ready["l2_go"], 1)

            def window_w(i, q, w):
                j = i * BODY + q
                if later(i, q, BODY, 2):
                    act.wait_ge(pa2.used, j - 1)
                sc.activation(xb[:, q % 2, :], row(xr, w), ACT.Copy)
                act.wait_ge(s_tr, j + 1)
                sc.activation(oht[:, q % 2, :], ps[:, q % 2, 0:P].bitcast(BF16), ACT.Copy).then_inc(s_trc, 1)
                if later(i, q, BODY, GROUP):
                    act.wait_ge(s_rm, 2 * H * (j - GROUP + 1))
                sc.activation(pen[:, q % GROUP, :, :], ohb[:, q % 2, :, :], ACT.Copy, scale=-LOW, bias=LOW).then_inc(s_pen, 1)

            def summed(i, q):
                j = i * BODY + q
                act.wait_ge(pa2.used, j + 1)
                if later(i, q, BODY, 2):
                    act.wait_ge(s_al, j - 1)
                sc.activation(zt[:, q % 2, :], ps[:, 2 + q % 2, 0:PAIR], ACT.Copy).then_inc(s_zc, 1)
                sc.activation(lt[:, q % 2, :], ps[:, 2 + q % 2, 0:PAIR], ACT.Copy, scale=0.2).then_inc(s_zc, 1)

            def logits(i, q):
                j = i * BODY + q
                act.wait_ge(s_al, j + 1)
                sc.activation(alpha[:, bass.ds(j, 1), :].rearrange("p a c -> p (a c)"),
                              ps[:, 4 + q % 4, 0:2 * H], ACT.Copy).then_inc(s_alc, 1)
            steps(act, NP, BODY, [(0, window_w), (1, summed), (3, logits)], (ET.Activation, bids[32:33, :], 0))

            act.wait_ge(s_rm, 2 * H * NP)
            for s in range(RING):
                act.wait_ge(s_kept[s], 16 * NP // RING)

            def fixmax(i, q):
                w = i * 2 + q
                if later(i, q, 2, 2):
                    act.wait_ge(s_rt, w - 1)
                sc.activation(rfix[:, q, :], row(rmax, w), ACT.Copy).then_inc(s_rc, 1)
            steps(act, NB - 1, 2, [(0, fixmax)])
            fixmax(NB // 2, 0)

            act.wait_ge(ready["l2_sums"], 1)

            def turned(i, q):
                j = i * BODY + q
                act.wait_ge(b_tr, j + 1)
                if later(i, q, BODY, 2):
                    act.wait_ge(b_sh, j - 1)
                sc.activation(oht[:, q % 2, 0:P].bitcast(BF16), ps[:, q % 2, 0:P].bitcast(BF16), ACT.Copy).then_inc(b_trc, 1)

            def weights(i, q):
                j = i * BODY + q
                act.wait_ge(b_sub, j + 1)
                if later(i, q, BODY, 2):
                    act.wait_ge(pb2.used, j - 1)
                sc.activation(ea8[:, q % 2, :], ea8[:, q % 2, :], ACT.Relu).then_inc(b_dif, 1)
                act.wait_ge(b_dif, j + 1)
                sc.activation(msg[:, q % 2, :, D:AW], ea8[:, q % 2, :].rearrange("p (t h) -> p t h", t=2),
                              ACT.Exp, scale=-1.0).then_inc(b_exp, 1)
            steps(act, NP, BODY, [(2, weights), (0, turned)])
            act.wait_ge(ready["l2_sums_done"], 1)
            sc.activation(eself, eself, ACT.Exp).then_inc(s_exs, 1)
            act.wait_ge(s_sq, 4)
            sc.activation(msg[:, 0, 1, 0:D], msg[:, 0, 0, 0:D], ACT.Sqrt).then_inc(s_sd, 1)
            act.wait_ge(ready["l2_norm"], 1)
            project_act(3, tmp, act)
            roots(4)
            act.wait_ge(ready["l3_in"], 1)
            project_act(4, x, act)

            act.wait_ge(ready["l3_rows"], 1)

            def turned3(i, q):
                j = i * BODY + q
                act.wait_ge(c_tr, j + 1)
                if later(i, q, BODY, 2):
                    act.wait_ge(c_z, j - 1)
                sc.activation(zt[0:2 * WD, q % 2, 0:P], ps[0:2 * WD, q % 2, 0:P], ACT.Copy).then_inc(c_trc, 1)

            def gelu(i, q):
                j = i * BODY + q
                act.wait_ge(c_z, j + 1)
                if later(i, q, BODY, 2):
                    act.wait_ge(pa3.used, j - 1)
                sc.activation(msg[:, q % 2, :, 0:D], ps[:, 2 + q % 2, 0:PAIR].rearrange("p (t f) -> p t f", t=2),
                              ACT.Gelu).then_inc(c_msg, 1)
            steps(act, NP, BODY, [(0, turned3), (1, gelu)])
            act.wait_ge(ready["l3_sums"], 1)
            project_act(5, acc[:, :, 0:D], act)
            roots(5)
            roots(6)

        @block.tensor
        def _(pe):
            mm = nc.tensor.matmul
            pe.wait_ge(s_load, 16 * 16)
            pe.wait_ge(s_const, CONSTS)
            for k in range(4):
                nc.tensor.transpose(ps[:, k, 0:P], wraw[:, k, :], ident[:]).then_inc(s_wt, 1)
            for order in range(2):
                pe.wait_ge(s_cnt, order + 1)
                if order:
                    pe.wait_ge(s_cmpr, 1)
                mm(ps[:, 4, 0:NB], ltri, cnt[:, 0:NB], start=True, stop=True)
                mm(ps[:, 5, 0:NB + 1], ones[:], cnt[:, 0:NB + 1], start=True, stop=True).then_inc(s_pre, 1)
                pe.wait_ge(s_cum, order + 1)
                mm(ps[0:NB, 6, 0:1], st[0:1, 2, 0:NB], ones[0:1, 0:1], start=True, stop=True)
                mm(ps[0:NB, 6, 1:2], st[0:1, 0, 0:NB], ones[0:1, 0:1], start=True, stop=True).then_inc(s_pre, 1)
                pe.wait_ge(s_cmp, order + 1)
                for n in range(2):
                    last = mm(ps[0:1, 4 + n, 0:NP // 2], ones[0:NB - 1, 0:1], mask[0:NB - 1, n * NP // 2:(n + 1) * NP // 2],
                              start=True, stop=True)
                if order:
                    pe.wait_ge(s_wtc, 4)
                    for n in range(2):
                        half = mask[0:NB - 1, n * NP // 2:(n + 1) * NP // 2]
                        mm(ps[:, n, 0:NP // 2], ones[0:NB - 1, :], half, start=True, stop=True)
                        last = mm(ps[0:1, 2 + n, 0:NP // 2], dinv[0:NB - 1, 0:1], half, start=True, stop=True)
                last.then_inc(s_cmpd, 1)

            def plain_pass(pas):
                def sums(i, q):
                    j = i * BODY + q
                    pe.wait_ge(pas.oh, j + 1)
                    pe.wait_ge(pas.got[q % RING], 32 * (turn(i, q, RING) + 1))
                    if later(i, q, BODY, 2):
                        pe.wait_ge(pas.acc, j - 1)
                    for u in range(2):
                        last = mm(ps[:, 6 + q % 2, 0:D + 1], oh[:, q % RING, u, :], g[:, q % RING, u, 0:D + 1],
                                  start=(u == 0), stop=(u == 1))
                    last.then_inc(pas.used, 1)
                steps(pe, NP, BODY, [(0, sums)])

            plain_pass(pa0)
            pe.wait_ge(s_wtc, 4)
            project_pe(0, w0t, D, None, pe)
            project_pe(1, w1, D, 0, pe)
            pe.wait_ge(ready["l1_rows"], 1)
            plain_pass(pa1)
            project_pe(2, wlrt, 2 * D, None, pe)

            pe.wait_ge(ready["l2_go"], 1)

            def turn_a(i, q):
                j = i * BODY + q
                pe.wait_ge(pa2.oh, j + 1)
                if later(i, q, BODY, 2):
                    pe.wait_ge(s_trc, j - 1)
                for u in range(2):
                    last = nc.tensor.transpose(ps[:, q % 2, 0:P].bitcast(BF16)[:, u * P:u * P + P], ohb[:, q % 2, u, :], identb[:])
                last.then_inc(s_tr, 1)

            def add(i, q):
                j = i * BODY + q
                pe.wait_ge(s_trc, j + 1)
                pe.wait_ge(pa2.got[q % RING], 32 * (turn(i, q, RING) + 1))
                if later(i, q, BODY, 2):
                    pe.wait_ge(s_zc, 2 * (j - 1))
                for u in range(2):
                    z = ps[:, 2 + q % 2, u * P:u * P + P]
                    mm(z, xb[:, q % 2, :], oht[:, q % 2, u * P:u * P + P], start=True, stop=False)
                    last = mm(z, g[:, q % RING, u, 0:D], ident[:], start=False, stop=True)
                last.then_inc(pa2.used, 1)

            def logit(i, q):
                j = i * BODY + q
                pe.wait_ge(s_lr, j + 1)
                if later(i, q, BODY, 4):
                    pe.wait_ge(s_alc, j - 3)
                    pe.wait_ge(s_rm, 2 * H * (j - 3))
                for u in range(2):
                    last = mm(ps[:, 4 + q % 4, u * H:u * H + H], lt[:, q % 2, u * P:u * P + P], attm[:],
                              start=True, stop=True)
                last.then_inc(s_al, 1)
            steps(pe, NP, BODY, [(3, logit), (0, turn_a), (1, add)])

            def turnmax(i, q):
                w = i * 2 + q
                pe.wait_ge(s_rc, w + 1)
                if later(i, q, 2, 2):
                    pe.wait_ge(s_rr, w - 1)
                for h in range(H):
                    last = nc.tensor.transpose(ps[:, q, h * P:h * P + P], rfix[:, q, h * P:h * P + P], ident[:])
                last.then_inc(s_rt, 1)
            steps(pe, NB - 1, 2, [(0, turnmax)])
            turnmax(NB // 2, 0)

            pe.wait_ge(ready["l2_sums"], 1)

            def turn_b(i, q):
                j = i * BODY + q
                pe.wait_ge(pb2.oh, j + 1)
                if later(i, q, BODY, 2):
                    pe.wait_ge(b_trc, j - 1)
                for u in range(2):
                    last = nc.tensor.transpose(ps[:, q % 2, 0:P].bitcast(BF16)[:, u * P:u * P + P], ohb[:, q % 2, u, :], identb[:])
                last.then_inc(b_tr, 1)

            def shift_w(i, q, w):
                j = i * BODY + q
                pe.wait_ge(b_trc, j + 1)
                if later(i, q, BODY, 2):
                    pe.wait_ge(b_sub, j - 1)
                for u in range(2):
                    for k in range(3):
                        last = mm(ps[:, 4 + q % 2, u * H:(u + 1) * H], oht[:, q % 2, 0:P].bitcast(BF16)[:, u * P:u * P + P],
                                  amax3[:, bass.ds(w, 1), k, :].rearrange("p a h -> p (a h)"), start=(k == 0), stop=(k == 2))
                last.then_inc(b_sh, 1)

            def sums_b(i, q):
                j = i * BODY + q
                pe.wait_ge(b_msg, j + 1)
                if later(i, q, BODY, 2):
                    pe.wait_ge(pb2.acc, j - 1)
                for u in range(2):
                    last = mm(ps[:, 6 + q % 2, 0:AW], oh[:, q % RING, u, :], msg[:, q % 2, u, :], start=(u == 0), stop=(u == 1))
                last.then_inc(pb2.used, 1)
            steps(pe, NP, BODY, [(3, sums_b), (1, shift_w), (0, turn_b)], (ET.PE, bids[32:33, :], 1))

            for n, t in enumerate((tmp, xr)):
                pe.wait_ge(s_bng, n + 1)
                for w in range(FULL + 1):
                    k = P if w < FULL else REST
                    last = mm(ps[:, 4 + n, 0:D], ones[0:k, :], t[0:k, w, :], start=(w == 0), stop=(w == FULL))
                last.then_inc(s_bn, 1)
            project_pe(3, lint, D, 1, pe)
            project_pe(4, w31, D, 2, pe)

            pe.wait_ge(ready["l3_rows"], 1)

            def turn_c(i, q):
                j = i * BODY + q
                if q % 2 == 0:
                    pe.wait_ge(pa3.rec[quad(q)], 16 * (turn(i, q, GROUP) + 1))
                if later(i, q, BODY, 2):
                    pe.wait_ge(c_trc, j - 1)
                nc.tensor.transpose(ps[0:2 * WD, q % 2, 0:P],
                                    rec[:, quad(q), 2 * (q % 2):2 * (q % 2) + 2, :].rearrange("p t w -> p (t w)"),
                                    ident[:]).then_inc(c_tr, 1)

            def hidden(i, q):
                j = i * BODY + q
                pe.wait_ge(c_trc, j + 1)
                pe.wait_ge(pa3.got[q % RING], 32 * (turn(i, q, RING) + 1))
                if later(i, q, BODY, 2):
                    pe.wait_ge(c_msg, j - 1)
                mm(ps[:, 2 + q % 2, 0:PAIR], zt[0:2 * WD, q % 2, 0:P], w31b[:].rearrange("p u f -> p (u f)"),
                   start=True, stop=False)
                mm(ps[:, 2 + q % 2, 0:PAIR], ident[:], g[:, q % RING, :, 0:D], start=False, stop=True).then_inc(c_z, 1)

            def sums_c(i, q):
                j = i * BODY + q
                pe.wait_ge(c_msg, j + 1)
                pe.wait_ge(pa3.oh, j + 1)
                if later(i, q, BODY, 2):
                    pe.wait_ge(pa3.acc, j - 1)
                for u in range(2):
                    last = mm(ps[:, 6 + q % 2, 0:D + 1], oh[:, q % RING, u, :], msg[:, q % 2, u, 0:D + 1],
                              start=(u == 0), stop=(u == 1))
                last.then_inc(pa3.used, 1)
            steps(pe, NP, BODY, [(0, turn_c), (1, hidden), (2, sums_c)])
            project_pe(5, w32, D, None, pe)

        @block.vector
        def _(dve):
            v = nc.vector

            def chain(done):
                chained = [0]

                def link(ins):
                    chained[0] += 1
                    ins.then_inc(done, 1)
                    dve.wait_ge(done, chained[0])
                return link
            link, link_general = chain(s_v), chain(s_vg)
            maski, scani, posi, keyi = (t.bitcast(I32) for t in (mask, scan, pos, key))

            def count(order, by, other, recx):
                v.tensor_scalar(maski, by, P - 1, None, ALU.bitwise_and)
                v.tensor_scalar(scani, by, 7, None, ALU.logical_shift_right)
                link(v.tensor_scalar(recx[:, :, 0:1].bitcast(I32).rearrange("p c w -> p (c w)"), other, N - 1, None, ALU.min))
                link(v.tensor_copy(recx[:, :, 1:2].rearrange("p c w -> p (c w)"), maski))
                if order:
                    link(v.tensor_copy(recx[:, :, 5:6].rearrange("p c w -> p (c w)"), by))
                link(v.tensor_copy(key, scani))
                for b in range(NB):
                    link(v.tensor_scalar(mask, key, float(b), 0.0, ALU.is_equal, ALU.add, accum_out=cnt[:, b:b + 1]))
                dve.sem_inc(s_cnt, 1)
                dve.wait_ge(s_pre, 2 * order + 1)
                sti = st[:, 0, 0:NB].bitcast(I32)
                if not order:
                    v.tensor_copy(unsorted[0:1, 0:1], ps[0:1, 5, NB:NB + 1]).then_inc(s_count, 1)
                link(v.tensor_scalar(sti, ps[:, 5, 0:NB], float(PAIR - 1), None, ALU.add))
                link(v.tensor_scalar(sti, sti, 8, None, ALU.logical_shift_right))
                link(v.tensor_copy(st[:, 1, 0:NB], sti))
                link(v.scalar_tensor_tensor(st[:, 0, 0:NB], st[:, 1, 0:NB], -float(PAIR), ps[:, 5, 0:NB], ALU.mult, ALU.add))
                link(v.tensor_tensor_scan(st[:, 2, 0:NB], ones[:, 0:NB], st[:, 1, 0:NB], 0.0, ALU.mult, ALU.add))
                v.tensor_tensor(st[:, 1, 0:NB], st[:, 2, 0:NB], st[:, 1, 0:NB], ALU.subtract).then_inc(s_cum, 1)
                dve.wait_ge(s_cum, order + 1)
                link(v.scalar_tensor_tensor(st[:, 3, 0:NB], st[:, 1, 0:NB], float(PAIR), ps[:, 4, 0:NB], ALU.mult, ALU.add))
                dve.wait_ge(s_pre, 2 * order + 2)
                link(v.tensor_copy(dinv[0:NB, 0:1], ps[0:NB, 6, 1:2]))
                v.tensor_scalar(mask[0:NB - 1, 0:NP], iotap[0:NB - 1, :], ps[0:NB - 1, 6, 0:1], None, ALU.is_ge).then_inc(s_cmp, 1)
                dve.wait_ge(s_cmpd, order + 1)
                for n in range(2):
                    last = v.tensor_copy(bids[32 * order:32 * order + 1, n * NP // 2:(n + 1) * NP // 2], ps[0:1, 4 + n, 0:NP // 2])
                last.then_inc(s_cmpr, 1)

            def rank(order, recx, words, link):
                link(v.memset(pos, 0.0))
                for part in range(PARTS):
                    c = slice(part * NC // PARTS, (part + 1) * NC // PARTS)
                    for b in range(NB):
                        link(v.tensor_scalar(mask[:, c], key[:, c], float(b), None, ALU.is_equal))
                        link(v.tensor_tensor_scan(scan[:, c], mask[:, c], mask[:, c], st[:, 3, b:b + 1], ALU.add, ALU.max))
                        if part < PARTS - 1:
                            v.tensor_copy(st[:, 3, b:b + 1], scan[:, c.stop - 1:c.stop])
                        link(v.copy_predicated(pos[:, c], maski[:, c], scan[:, c]))
                    link(v.tensor_scalar(scani[:, c], pos[:, c], -1.0, None, ALU.add))
                    v.tensor_scalar(maski[:, c], scani[:, c], PAIR - 1, 1, ALU.bitwise_and, ALU.logical_shift_right)
                    v.tensor_scalar(posi[:, c], scani[:, c], 8, 1, ALU.logical_shift_right, ALU.logical_shift_left)
                    link(v.tensor_scalar(keyi[:, c], scani[:, c], 1, None, ALU.bitwise_and))
                    link(v.tensor_tensor(posi[:, c], posi[:, c], keyi[:, c], ALU.bitwise_or))
                    v.scalar_tensor_tensor(recx[:, c, words - 1:words].bitcast(I32).rearrange("p c w -> p (c w)"), maski[:, c],
                                           float(T), posi[:, c], ALU.mult, ALU.add).then_inc(s_rank[order], 1)
                    dve.wait_ge(s_rank[order], part + 1)

            dve.wait_ge(s_edges, 128)
            dve.wait_ge(s_fill, FILLS)
            dve.wait_ge(s_const, CONSTS)
            dve.wait_ge(s_load, 16 * 16)
            v.tensor_copy(iotab[:], iota[:])
            v.tensor_copy(identb[:], ident[:])
            link(v.tensor_tensor(mask[:, 0:NC - 1], dsti[:, 0:NC - 1], dsti[:, 1:NC], ALU.is_gt))
            link(v.tensor_tensor(mask[:, NC - 1:NC], dsti[:, NC - 1:NC], nexti[:], ALU.is_gt))
            link(v.tensor_reduce(cnt[:, NB:NB + 1], mask, AX.X, ALU.add))
            count(0, srci, dsti, recs)
            rank(0, recs, WS, link)
            count(1, dsti, srci, recd)
            dve.wait_ge(s_eac, 3)
            for n in range(2):
                half = slice(n * NP // 2, (n + 1) * NP // 2)
                link(v.tensor_scalar(base[:, half], ps[:, n, 0:NP // 2], float(P), None, ALU.mult))
                link(v.scalar_tensor_tensor(mask[0:1, half], iotap[0:1, half], float(PAIR), ps[0:1, 2 + n, 0:NP // 2], ALU.mult, ALU.add))
            v.tensor_scalar(bids[96:97, :], mask[0:1, 0:NP], float(P * NC), None, ALU.min).then_inc(s_first, 1)
            dve.wait_ge(s_first, 1)
            with dve.If(is_unsorted(dve, ET.DVE) < 1):
                v.memset(fix[:, 0, 0:2, 0:5], 0.0).then_inc(s_empty, 1)
                v.memset(fix[:, 0, 0:2, 6:WD], 0.0).then_inc(s_empty, 1)
                v.memset(fix[:, 0, 0:2, 5:6], 1e6).then_inc(s_empty, 1)

                def place(i, h):
                    dve.wait_ge(s_run[h], 64 * (i + 1))
                    v.tensor_tensor(fix[:, h, :, 1:2].rearrange("p (k t) w -> p k (t w)", k=4),
                                    fix[:, h, :, 5:6].rearrange("p (k t) w -> p k (t w)", k=4),
                                    base[:, bass.ds(i * 8 + 4 * h, 4)].unsqueeze(2).to_broadcast([P, 4, 2]),
                                    ALU.subtract).then_inc(s_node, 1)
                steps(dve, NP // 4, 2, [(0, place)])
            with dve.Else():
                rank(1, recd, WD, link_general)
                dve.wait_ge(s_filled_dst, 16 * FILLERS)
            dve.wait_ge(s_filled, 16 * FILLERS)
            v.memset(x[:], 0.0).then_inc(ready["x_zero"], 1)
            v.memset(acc, 0.0)
            link(v.memset(st[:], 0.0))

            def onehots(pas, words, free, turned=None):
                def onehot(i, q):
                    if q % 2 == 0:
                        dve.wait_ge(pas.rec[quad(q)], 16 * (turn(i, q, GROUP) + 1))
                    if later(i, q, BODY, RING):
                        free(i * BODY + q - RING + 1)
                    if turned is not None and later(i, q, BODY, 2):
                        dve.wait_ge(turned, i * BODY + q - 1)
                    for u in range(2):
                        node = record(quad(q), 2 * (q % 2) + u, words)[:, 1:2]
                        if turned is not None:
                            v.tensor_scalar(ohb[:, q % 2, u, :], iotab[:], node, None, ALU.is_equal)
                        last = v.tensor_scalar(oh[:, q % RING, u, :], iota[:], node, None, ALU.is_equal)
                    last.then_inc(pas.oh, 1)
                return onehot

            def adds(pas, width):
                def add_w(i, q, w):
                    j = i * BODY + q
                    dve.wait_ge(pas.used, j + 1)
                    if later(i, q, BODY, 1):
                        dve.wait_ge(pas.acc, j)
                    v.tensor_tensor(row(acc, w)[:, 0:width], row(acc, w)[:, 0:width], ps[:, 6 + q % 2, 0:width],
                                    ALU.add).then_inc(pas.acc, 1)
                return add_w

            def plain_pass(pas, words, order, lag):
                free = lambda n: dve.wait_ge(pas.used, n)
                steps(dve, NP, BODY, [(0, onehots(pas, words, free)), (lag, adds(pas, D + 1))],
                      (ET.DVE, bids[32 * order:32 * order + 1, :], lag))
                dve.wait_ge(pas.acc, NP)

            wide = [P, NW, D]
            by_window = lambda t: t.unsqueeze(2).to_broadcast(wide)
            by_feature = lambda t: t.unsqueeze(1).to_broadcast(wide)
            sd = [0]

            def rooted():
                sd[0] += 1
                dve.wait_ge(s_sd, sd[0])

            def layernorm():
                link(v.tensor_reduce(st[:, 0, :], x[:], AX.X, ALU.add))
                link(v.tensor_scalar(st[:, 1, :], st[:, 0, :], -1.0 / D, None, ALU.mult))
                link(v.tensor_tensor(x[:], x[:], by_window(st[:, 1, :]), ALU.add))
                link(v.tensor_tensor(tmp, x[:], x[:], ALU.mult))
                link(v.tensor_reduce(st[:, 0, :], tmp, AX.X, ALU.add))
                v.tensor_scalar(st[:, 2, :], st[:, 0, :], 1.0 / D, EPS, ALU.mult, ALU.add).then_inc(s_sq, 1)
                rooted()
                link(v.reciprocal(st[:, 1, :], st[:, 3, :]))
                link(v.tensor_tensor(x[:], x[:], by_window(st[:, 1, :]), ALU.mult))

            plain_pass(pa0, WS, 0, 1)
            column = acc[:, :, ONE:ONE + 1].rearrange("p w a -> p (w a)")
            link(v.tensor_scalar(st[:, 0, :], column, 1.0, None, ALU.max))
            v.tensor_scalar(st[:, 2, :], column, 1.0, None, ALU.add).then_inc(s_sq, 1)
            link(v.reciprocal(st[:, 1, :], st[:, 0, :]))
            v.tensor_tensor(acc[:, :, 0:D], acc[:, :, 0:D], by_window(st[:, 1, :]), ALU.mult).then_inc(ready["l0_mean"], 1)
            rooted()
            link(v.reciprocal(dinv[:], st[:, 3, :]))
            dve.wait_ge(s_x, 32)
            dve.wait_ge(s_vec, 16)
            link(v.tensor_tensor(x[:], x[:], by_feature(bc[:, 0, :]), ALU.add))
            project_dve(0, [x], dve, add=True)
            dve.wait_ge(s_pe, NW)
            layernorm()
            dve.sem_inc(ready["l1_in"], 1)
            link(v.memset(acc, 0.0))
            project_dve(1, [xr], dve, scale=dinv)
            dve.wait_ge(s_pe, 2 * NW)
            dve.sem_inc(ready["l1_rows"], 1)
            plain_pass(pa1, WS, 0, 1)
            link(v.tensor_tensor(acc[:, :, 0:D], acc[:, :, 0:D], xr[:], ALU.add))
            link(v.tensor_tensor(acc[:, :, 0:D], acc[:, :, 0:D], by_window(dinv[:]), ALU.mult))
            link(v.tensor_tensor(x[:], x[:], acc[:, :, 0:D], ALU.add))
            layernorm()
            dve.sem_inc(ready["l2_in"], 1)
            dve.wait_ge(s_vec, 48)
            project_dve(2, [tmp, xr], dve, bias=bc)
            dve.wait_ge(s_pe, 3 * NW)
            v.tensor_tensor(zself, tmp, xr[:], ALU.add).then_inc(ready["l2_left"], 1)
            dve.wait_ge(ready["l2_left"], 1)
            link(v.scalar_tensor_tensor(zself, zself, 0.2, zself, ALU.mult, ALU.max))
            dve.wait_ge(s_vec, 64)
            link(v.tensor_tensor(zself, zself, by_feature(bc[:, 0, :]), ALU.mult))
            link(v.tensor_reduce(aself[:], big[:, 0:NW * D].rearrange("p (h c) -> p h c", c=C), AX.X, ALU.add))
            v.memset(rmax, LOW).then_inc(ready["l2_go"], 1)
            dve.wait_ge(ready["l2_go"], 1)

            def leaky(i, q):
                j = i * BODY + q
                dve.wait_ge(s_zc, 2 * (j + 1))
                v.tensor_tensor(lt[:, q % 2, :], zt[:, q % 2, :], lt[:, q % 2, :], ALU.max).then_inc(s_lr, 1)

            def onehot_bf(i, q):
                j = i * BODY + q
                if q % 2 == 0:
                    dve.wait_ge(pa2.rec[quad(q)], 16 * (turn(i, q, GROUP) + 1))
                if later(i, q, BODY, 2):
                    dve.wait_ge(s_tr, j - 1)
                    dve.wait_ge(s_pen, j - 1)
                for u in range(2):
                    node = record(quad(q), 2 * (q % 2) + u, WD)[:, 1:2]
                    last = v.tensor_scalar(ohb[:, q % 2, u, :], iotab[:], node, None, ALU.is_equal)
                last.then_inc(pa2.oh, 1)

            def maxima_w(i, q, w):
                j = i * BODY + q
                dve.wait_ge(s_pen, j + 1)
                dve.wait_ge(s_alc, j + 1)
                for u in range(2):
                    for h in range(H):
                        if u or later(i, q, BODY, 1):
                            dve.wait_ge(s_rm, 2 * H * j + H * (u - 1) + h + 1)
                        r = row(rmax, w)[:, h * P:h * P + P]
                        v.scalar_tensor_tensor(r, pen[:, q % GROUP, u, :], ps[:, 4 + q % 4, u * H + h:u * H + h + 1], r,
                                               ALU.add, ALU.max).then_inc(s_rm, 1)
            steps(dve, NP, BODY, [(0, onehot_bf), (2, leaky), (4, maxima_w)], (ET.DVE, bids[32:33, :], 4))

            rest = msg[:].rearrange("p a u f -> p (a u f)")[:, 0:NW * H]
            rest3 = rest.rearrange("p (w h) -> p w h", h=H)

            def reduce(i, q):
                w = i * 2 + q
                dve.wait_ge(s_rt, w + 1)
                v.tensor_reduce(amax[:, bass.ds(w * H, H)], ps[:, q, :].rearrange("p (h e) -> p h e", h=H), AX.X, ALU.max)\
                    .then_inc(s_rr, 1)
            link(v.memset(amax[:], LOW))
            steps(dve, NB - 1, 2, [(0, reduce)])
            reduce(NB // 2, 0)
            dve.wait_ge(s_rr, NB)
            link(v.tensor_tensor(amax[:], amax[:], aself[:], ALU.max))
            link(v.tensor_copy(rest, amax[:]))
            for k in range(3):
                part = amax3[:, :, k, :]
                link(v.tensor_copy(part, rest3))
                if k < 2:
                    link(v.tensor_tensor(rest3, rest3, part, ALU.subtract))
            v.memset(acc, 0.0).then_inc(ready["l2_sums"], 1)
            dve.wait_ge(ready["l2_sums"], 1)

            def shifted(i, q):
                j = i * BODY + q
                dve.wait_ge(b_sh, j + 1)
                if later(i, q, BODY, 2):
                    dve.wait_ge(b_exp, j - 1)
                v.tensor_tensor(ea8[:, q % 2, :], ps[:, 4 + q % 2, 0:2 * H], alpha[:, bass.ds(j, 1), :].rearrange("p a c -> p (a c)"),
                                ALU.subtract).then_inc(b_sub, 1)

            def messages(i, q):
                j = i * BODY + q
                dve.wait_ge(b_exp, j + 1)
                dve.wait_ge(pb2.got[q % RING], 16 * (turn(i, q, RING) + 1))
                for u in range(2):
                    last = v.tensor_tensor(msg[:, q % 2, u, 0:D].rearrange("p (h c) -> p h c", h=H),
                                           g[:, q % RING, u, 0:D].rearrange("p (h c) -> p h c", h=H),
                                           msg[:, q % 2, u, D:AW].unsqueeze(2).to_broadcast([P, H, C]), ALU.mult)
                last.then_inc(b_msg, 1)
            steps(dve, NP, BODY, [(3, messages), (2, shifted), (0, onehots(pb2, WD, lambda n: dve.wait_ge(pb2.used, n), b_tr)),
                                  (4, adds(pb2, AW))], (ET.DVE, bids[32:33, :], 4))
            dve.wait_ge(pb2.acc, NP)
            v.tensor_tensor(eself, aself[:], amax[:], ALU.subtract).then_inc(ready["l2_sums_done"], 1)
            heads = lambda t: t.rearrange("p w (h c) -> p (w h) c", c=C)
            by_head = lambda t: t.unsqueeze(2).to_broadcast([P, NW * H, C])
            dve.wait_ge(s_exs, 1)
            dve.wait_ge(s_tab, 48)
            link(v.tensor_tensor(heads(tmp), heads(tmp), by_head(eself), ALU.mult))
            link(v.tensor_tensor(tmp, tmp, acc[:, :, 0:D], ALU.add))
            e3 = eself.rearrange("p (w h) -> p w h", h=H)
            link(v.tensor_tensor(e3, e3, acc[:, :, D:AW], ALU.add))
            link(v.tensor_scalar(eself, eself, 1e-16, None, ALU.add))
            link(v.reciprocal(eself, eself))
            link(v.tensor_tensor(heads(tmp), heads(tmp), by_head(eself), ALU.mult))
            dve.wait_ge(s_vec, 96)
            v.tensor_tensor(tmp, tmp, by_feature(bc[:, 0, :]), ALU.add).then_inc(ready["l2_conv_bias_used"], 1)
            dve.wait_ge(ready["l2_conv_bias_used"], 1)
            v.tensor_scalar(tmp, tmp, 0.0, None, ALU.max).then_inc(s_bng, 1)
            dve.wait_ge(s_bn, 1)
            mean, var, root = msg[:, 1, 0, 0:D], msg[:, 0, 0, 0:D], msg[:, 0, 1, 0:D]
            link(v.tensor_scalar(mean, ps[:, 4, 0:D], 1.0 / N, None, ALU.mult))
            link(v.tensor_tensor(tmp, tmp, by_feature(mean), ALU.subtract))
            v.tensor_tensor(xr[:], tmp, tmp, ALU.mult).then_inc(s_bng, 1)
            dve.wait_ge(s_bn, 2)
            v.tensor_scalar(var, ps[:, 5, 0:D], 1.0 / N, EPS, ALU.mult, ALU.add).then_inc(s_sq, 1)
            rooted()
            link(v.reciprocal(var, root))
            link(v.tensor_tensor(var, var, bc[:, 1, :], ALU.mult))
            link(v.tensor_tensor(tmp, tmp, by_feature(var), ALU.mult))
            dve.wait_ge(s_vec, 112)
            v.tensor_tensor(tmp, tmp, by_feature(bc[:, 0, :]), ALU.add).then_inc(ready["l2_norm"], 1)
            project_dve(3, [x], dve, add=True)
            dve.wait_ge(s_pe, 4 * NW)
            layernorm()
            dve.sem_inc(ready["l3_in"], 1)
            link(v.memset(acc, 0.0))
            link(v.memset(msg[:, :, :, ONE:ONE + 1], 1.0))
            project_dve(4, [xr], dve)
            dve.wait_ge(s_pe, 5 * NW)
            dve.wait_ge(ready["l3_in"], 1)
            v.memset(st[:, 0, :], 0.0).then_inc(ready["l3_rows"], 1)
            plain_pass(pa3, WD, 1, 3)
            v.memset(st[:, 0, :], 0.0).then_inc(ready["l3_sums"], 1)
            project_dve(5, [tmp], dve)
            dve.wait_ge(s_pe, 6 * NW)
            dve.wait_ge(s_vec, 144)
            link(v.tensor_copy(st[:, 1, :], column))
            link(v.tensor_copy(zself, x[:]))
            v.tensor_tensor(x[:], x[:], tmp, ALU.add)
            link(v.tensor_tensor(xr[:], by_window(st[:, 1, :]), by_feature(bc[:, 0, :]), ALU.mult))
            v.tensor_tensor(x[:], x[:], xr[:], ALU.add).then_inc(ready["l3_b2_used"], 1)
            dve.wait_ge(ready["l3_b2_used"], 1)
            layernorm()
            link(v.tensor_tensor(x[:], x[:], by_feature(bc[:, 1, :]), ALU.mult))
            dve.wait_ge(s_vec, 160)
            link(v.tensor_tensor(x[:], x[:], by_feature(bc[:, 0, :]), ALU.add))
            link(v.tensor_tensor(x[:], x[:], zself, ALU.add))
            layernorm()
            v.memset(st[:, 0, :], 0.0).then_inc(ready["out"], 1)


_INS = ["x", "src", "dst", "edge_attr_3", "L0_gnn_x_clique", "L0_gnn_W", "L0_gnn_b", "L1_gnn_W", "L1_gnn_b",
        "L2_gnn_lin_l_w", "L2_gnn_lin_l_b", "L2_gnn_lin_r_w", "L2_gnn_lin_r_b", "L2_gnn_att", "L2_gnn_conv_bias",
        "L2_gnn_lin_w", "L2_gnn_lin_b", "L2_gnn_bn_gamma", "L2_gnn_bn_beta", "L3_gnn_W1", "L3_gnn_b1", "L3_gnn_W2",
        "L3_gnn_b2", "L3_gnn_gamma", "L3_gnn_beta"]


def kernel(**inputs):
    import numpy as _np
    import concourse.bacc as _bacc
    from concourse import mybir as _mybir
    from concourse.bass_utils import run_bass_kernel_spmd as _run

    nc = _bacc.Bacc("TRN2", target_bir_lowering=False, num_devices=1)
    arrays, args = {}, {}
    for name in _INS:
        arr = _np.ascontiguousarray(inputs[name])
        arrays[f"in_{name}"] = arr
        args[name] = nc.dram_tensor(f"in_{name}", arr.shape, _mybir.dt.from_np(arr.dtype), kind="ExternalInput").ap()
    out = nc.dram_tensor("out_0", (N, D), F32, kind="ExternalOutput").ap()
    gnn_kernel(nc, args, out)
    r = _run(nc, [arrays], core_ids=[0])
    return r.results[0]["out_0"]
```
